# Optimizing a Trainium2 kernel written in Bass

```python
import numpy as np
import jax
import jax.numpy as jnp

def _softmax(x, axis=-1):
    return jax.nn.softmax(x, axis=axis)

def _gelu(x):
    return jax.nn.gelu(x, approximate=True)

def _silu(x):
    return jax.nn.silu(x)

def _sigmoid(x):
    return jax.nn.sigmoid(x)

def _layernorm(x, axis=-1, eps=1e-05):
    m = jnp.mean(x, axis=axis, keepdims=True)
    v = jnp.var(x, axis=axis, keepdims=True)
    return (x - m) / jnp.sqrt(v + eps)

def _scatter_add(tgt, idx, src, axis=0):
    return tgt.at[idx].add(src)

def _segment_sum(src, seg, n):
    return jax.ops.segment_sum(src, seg, n)
kernel_name = 'mk_xattn_seq_d2_seqx_r4_c8d475'

def setup_inputs(seed: int=0):
    np.random.seed(seed)
    _w = jnp.asarray

    def _rec_inputs():
        import jax
        import jax.numpy as jnp
        _rk = jax.random.key(seed)
        x = -0.0003929 + 0.9999 * jax.random.normal(jax.random.fold_in(_rk, 1), (16, 100, 512), jnp.float32)
        _lenS = 100 - jax.random.randint(jax.random.fold_in(_rk, 7), (16,), 0, max(1, 100 // 4) + 1, jnp.int32)
        _lenS2 = 361 - jax.random.randint(jax.random.fold_in(_rk, 8), (16,), 0, max(1, 361 // 4) + 1, jnp.int32)
        _ctx_2048P = jax.random.normal(jax.random.fold_in(_rk, 11), (16, 16, 512), jnp.float32)
        _ctx_2048c = jax.random.dirichlet(jax.random.fold_in(_rk, 511), 0.3 * jnp.ones((16,), jnp.float32), (16, 361))
        _ctx_2048t = jnp.einsum('bsk,bkd->bsd', _ctx_2048c, _ctx_2048P)
        _ctx_2048t = _ctx_2048t * jax.lax.rsqrt(jnp.mean(jnp.square(_ctx_2048t)) + 1e-12) * 0.953939
        ctx_2048 = -8.57375e-05 + 0.999917 * (_ctx_2048t + 0.3 * jax.random.normal(jax.random.fold_in(_rk, 611), (16, 361, 512), jnp.float32))
        _validS = jnp.arange(100)[None, :] < _lenS[:, None]
        _validS2 = jnp.arange(361)[None, :] < _lenS2[:, None]
        _causal = jnp.tril(jnp.ones((100, 100), dtype=bool))
        mask_BxS2_bf1 = jnp.ones((16, 361), dtype=bool)
        return (x, ctx_2048, mask_BxS2_bf1)
    x, ctx_2048, mask_BxS2_bf1 = _rec_inputs()

    def _L0_xattn_setup():
        import jax, jax.numpy as jnp
        import numpy as np
        HIDDEN = 512
        HEADS = 16
        HEAD_DIM = HIDDEN // HEADS
        LN_EPS = 1e-05
        GATE_INIT = 0.5

        def _layer_norm(x, gamma, beta):
            mu = jnp.mean(x, axis=-1, keepdims=True)
            var = jnp.mean(jnp.square(x - mu), axis=-1, keepdims=True)
            return (x - mu) * jax.lax.rsqrt(var + LN_EPS) * gamma + beta
        key = jax.random.key(seed)
        ks = jax.random.split(key, 8)
        B, T_TEXT, T_AUDIO = (4, 512, 375)
        s = 0.02
        return {'hidden_states': jax.random.normal(ks[0], (B, T_TEXT, HIDDEN), jnp.float32), 'audio_kv': jax.random.normal(ks[1], (B, T_AUDIO, HIDDEN), jnp.float32), 'audio_attention_mask': jnp.ones((B, T_AUDIO), dtype=bool), 'Wq': jax.random.normal(ks[2], (HIDDEN, HIDDEN), jnp.float32) * s, 'Wk': jax.random.normal(ks[3], (HIDDEN, HIDDEN), jnp.float32) * s, 'Wv': jax.random.normal(ks[4], (HIDDEN, HIDDEN), jnp.float32) * s, 'Wo': jax.random.normal(ks[5], (HIDDEN, HIDDEN), jnp.float32) * s, 'ln_gamma': jnp.ones((HIDDEN,), jnp.float32), 'ln_beta': jnp.zeros((HIDDEN,), jnp.float32), 'gate': jnp.array([GATE_INIT], jnp.float32)}
    _L0_xattn_all = _L0_xattn_setup()
    _L0_xattn_in = {k: v for k, v in _L0_xattn_all.items() if k in ('Wq', 'Wk', 'Wv', 'Wo', 'ln_gamma', 'ln_beta', 'gate')}
    del _L0_xattn_all

    def _L1_xattn_setup():
        import jax, jax.numpy as jnp
        import numpy as np
        D = 512
        H = 16
        HD = D // H
        INNER = 4 * D
        EPS = 1e-05

        def layer_norm(x, w, b):
            mu = jnp.mean(x, axis=-1, keepdims=True)
            var = jnp.mean(jnp.square(x - mu), axis=-1, keepdims=True)
            return (x - mu) * jax.lax.rsqrt(var + EPS) * w + b
        key = jax.random.key(seed)
        ks = jax.random.split(key, 12)
        B, LQ, LK = (4, 256, 512)
        std = 0.02
        inp = {'hidden_states': jax.random.normal(ks[0], (B, LQ, D), jnp.float32), 'encoder_hidden_states': jax.random.normal(ks[1], (B, LK, D), jnp.float32), 'encoder_attention_mask': jnp.ones((B, LK), dtype=bool), 'ln1_w': jnp.ones((D,), jnp.float32), 'ln1_b': jnp.zeros((D,), jnp.float32), 'q_w': jax.random.normal(ks[2], (D, D), jnp.float32) * std, 'q_b': jnp.zeros((D,), jnp.float32), 'k_w': jax.random.normal(ks[3], (D, D), jnp.float32) * std, 'k_b': jnp.zeros((D,), jnp.float32), 'v_w': jax.random.normal(ks[4], (D, D), jnp.float32) * std, 'v_b': jnp.zeros((D,), jnp.float32), 'cproj_w': jax.random.normal(ks[5], (D, D), jnp.float32) * std, 'cproj_b': jnp.zeros((D,), jnp.float32), 'ln2_w': jnp.ones((D,), jnp.float32), 'ln2_b': jnp.zeros((D,), jnp.float32), 'fc_w': jax.random.normal(ks[6], (D, INNER), jnp.float32) * std, 'fc_b': jnp.zeros((INNER,), jnp.float32), 'proj_w': jax.random.normal(ks[7], (INNER, D), jnp.float32) * std, 'proj_b': jnp.zeros((D,), jnp.float32)}
        return inp
    _L1_xattn_all = _L1_xattn_setup()
    _L1_xattn_in = {k: v for k, v in _L1_xattn_all.items() if k in ('ln1_w', 'ln1_b', 'q_w', 'q_b', 'k_w', 'k_b', 'v_w', 'v_b', 'cproj_w', 'cproj_b', 'ln2_w', 'ln2_b', 'fc_w', 'fc_b', 'proj_w', 'proj_b')}
    del _L1_xattn_all
    return {'x': x, 'ctx_2048': ctx_2048, 'mask_BxS2_bf1': mask_BxS2_bf1, 'L0_xattn_Wq': _L0_xattn_in['Wq'], 'L0_xattn_Wk': _L0_xattn_in['Wk'], 'L0_xattn_Wv': _L0_xattn_in['Wv'], 'L0_xattn_Wo': _L0_xattn_in['Wo'], 'L0_xattn_ln_gamma': _L0_xattn_in['ln_gamma'], 'L0_xattn_ln_beta': _L0_xattn_in['ln_beta'], 'L0_xattn_gate': _L0_xattn_in['gate'], 'L1_xattn_ln1_w': _L1_xattn_in['ln1_w'], 'L1_xattn_ln1_b': _L1_xattn_in['ln1_b'], 'L1_xattn_q_w': _L1_xattn_in['q_w'], 'L1_xattn_q_b': _L1_xattn_in['q_b'], 'L1_xattn_k_w': _L1_xattn_in['k_w'], 'L1_xattn_k_b': _L1_xattn_in['k_b'], 'L1_xattn_v_w': _L1_xattn_in['v_w'], 'L1_xattn_v_b': _L1_xattn_in['v_b'], 'L1_xattn_cproj_w': _L1_xattn_in['cproj_w'], 'L1_xattn_cproj_b': _L1_xattn_in['cproj_b'], 'L1_xattn_ln2_w': _L1_xattn_in['ln2_w'], 'L1_xattn_ln2_b': _L1_xattn_in['ln2_b'], 'L1_xattn_fc_w': _L1_xattn_in['fc_w'], 'L1_xattn_fc_b': _L1_xattn_in['fc_b'], 'L1_xattn_proj_w': _L1_xattn_in['proj_w'], 'L1_xattn_proj_b': _L1_xattn_in['proj_b']}

def reference(x, ctx_2048, mask_BxS2_bf1, L0_xattn_Wq, L0_xattn_Wk, L0_xattn_Wv, L0_xattn_Wo, L0_xattn_ln_gamma, L0_xattn_ln_beta, L0_xattn_gate, L1_xattn_ln1_w, L1_xattn_ln1_b, L1_xattn_q_w, L1_xattn_q_b, L1_xattn_k_w, L1_xattn_k_b, L1_xattn_v_w, L1_xattn_v_b, L1_xattn_cproj_w, L1_xattn_cproj_b, L1_xattn_ln2_w, L1_xattn_ln2_b, L1_xattn_fc_w, L1_xattn_fc_b, L1_xattn_proj_w, L1_xattn_proj_b):
    import jax
    import jax.numpy as jnp

    def _L0_xattn_ref(hidden_states, audio_kv, audio_attention_mask, Wq, Wk, Wv, Wo, ln_gamma, ln_beta, gate):
        import jax, jax.numpy as jnp
        import numpy as np
        HIDDEN = 512
        HEADS = 16
        HEAD_DIM = HIDDEN // HEADS
        LN_EPS = 1e-05
        GATE_INIT = 0.5

        def _layer_norm(x, gamma, beta):
            mu = jnp.mean(x, axis=-1, keepdims=True)
            var = jnp.mean(jnp.square(x - mu), axis=-1, keepdims=True)
            return (x - mu) * jax.lax.rsqrt(var + LN_EPS) * gamma + beta
        B, Tt, D = hidden_states.shape
        Ta = audio_kv.shape[1]
        scale = HEAD_DIM ** (-0.5)
        a = _layer_norm(audio_kv, ln_gamma, ln_beta)
        Q = (hidden_states @ Wq.T).reshape(B, Tt, HEADS, HEAD_DIM).transpose(0, 2, 1, 3)
        K = (a @ Wk.T).reshape(B, Ta, HEADS, HEAD_DIM).transpose(0, 2, 1, 3)
        V = (a @ Wv.T).reshape(B, Ta, HEADS, HEAD_DIM).transpose(0, 2, 1, 3)
        scores = jnp.einsum('bhtd,bhsd->bhts', Q, K) * scale
        mask = audio_attention_mask[:, None, None, :]
        scores = jnp.where(mask, scores, jnp.float32(-jnp.inf))
        attn = jax.nn.softmax(scores, axis=-1)
        out = jnp.einsum('bhts,bhsd->bhtd', attn, V)
        out = out.transpose(0, 2, 1, 3).reshape(B, Tt, D)
        out = out @ Wo.T
        return hidden_states + jnp.tanh(gate) * out

    def _L1_xattn_ref(hidden_states, encoder_hidden_states, encoder_attention_mask, ln1_w, ln1_b, q_w, q_b, k_w, k_b, v_w, v_b, cproj_w, cproj_b, ln2_w, ln2_b, fc_w, fc_b, proj_w, proj_b):
        import jax, jax.numpy as jnp
        import numpy as np
        D = 512
        H = 16
        HD = D // H
        INNER = 4 * D
        EPS = 1e-05

        def layer_norm(x, w, b):
            mu = jnp.mean(x, axis=-1, keepdims=True)
            var = jnp.mean(jnp.square(x - mu), axis=-1, keepdims=True)
            return (x - mu) * jax.lax.rsqrt(var + EPS) * w + b
        B, LQ, _ = hidden_states.shape
        LK = encoder_hidden_states.shape[1]
        residual = hidden_states
        x = layer_norm(hidden_states, ln1_w, ln1_b)
        q = (x @ q_w + q_b).reshape(B, LQ, H, HD).transpose(0, 2, 1, 3)
        k = (encoder_hidden_states @ k_w + k_b).reshape(B, LK, H, HD).transpose(0, 2, 1, 3)
        v = (encoder_hidden_states @ v_w + v_b).reshape(B, LK, H, HD).transpose(0, 2, 1, 3)
        scale = 1.0 / np.sqrt(HD).astype(np.float32)
        scores = jnp.einsum('bhqd,bhkd->bhqk', q, k) * scale
        mask = encoder_attention_mask[:, None, None, :]
        mask_value = jnp.finfo(scores.dtype).min
        scores = jnp.where(mask, scores, mask_value)
        attn = jax.nn.softmax(scores, axis=-1)
        out = jnp.einsum('bhqk,bhkd->bhqd', attn, v)
        out = out.transpose(0, 2, 1, 3).reshape(B, LQ, D)
        out = out @ cproj_w + cproj_b
        hidden = out + residual
        residual = hidden
        y = layer_norm(hidden, ln2_w, ln2_b)
        y = jax.nn.gelu(y @ fc_w + fc_b, approximate=True)
        y = y @ proj_w + proj_b
        return residual + y
    x = _L0_xattn_ref(x, ctx_2048, mask_BxS2_bf1, L0_xattn_Wq, L0_xattn_Wk, L0_xattn_Wv, L0_xattn_Wo, L0_xattn_ln_gamma, L0_xattn_ln_beta, L0_xattn_gate)
    x = _L1_xattn_ref(x, ctx_2048, mask_BxS2_bf1, L1_xattn_ln1_w, L1_xattn_ln1_b, L1_xattn_q_w, L1_xattn_q_b, L1_xattn_k_w, L1_xattn_k_b, L1_xattn_v_w, L1_xattn_v_b, L1_xattn_cproj_w, L1_xattn_cproj_b, L1_xattn_ln2_w, L1_xattn_ln2_b, L1_xattn_fc_w, L1_xattn_fc_b, L1_xattn_proj_w, L1_xattn_proj_b)
    return x

_drawn_inputs = setup_inputs


def setup_inputs(seed=0):
    import zlib

    import numpy as np

    out = dict(_drawn_inputs(seed))
    spreads = {'L0_xattn_ln_gamma': (1.0, 0.6),
     'L0_xattn_ln_beta': (0.0, 0.8),
     'L1_xattn_ln1_w': (1.0, 0.6),
     'L1_xattn_ln1_b': (0.0, 0.8),
     'L1_xattn_q_b': (0.0, 0.8),
     'L1_xattn_k_b': (0.0, 0.8),
     'L1_xattn_v_b': (0.0, 0.1),
     'L1_xattn_cproj_b': (0.0, 0.1),
     'L1_xattn_ln2_w': (1.0, 0.2),
     'L1_xattn_ln2_b': (0.0, 0.335),
     'L1_xattn_fc_b': (0.0, 0.1),
     'L1_xattn_proj_b': (0.0, 0.1)}
    factors = {'L0_xattn_Wq': 8.0, 'L0_xattn_Wk': 8.0, 'L1_xattn_q_w': 7.415, 'L1_xattn_k_w': 7.275}
    for name, (base, spread) in spreads.items():
        noise = np.random.default_rng([zlib.crc32(name.encode()), seed]).standard_normal(out[name].shape)
        drawn = base * np.exp(spread * noise) if base else spread * noise
        out[name] = jnp.asarray(drawn.astype(out[name].dtype))
    for name, factor in factors.items():
        out[name] = (out[name] * factor).astype(out[name].dtype)
    return out
```

```python
from contextlib import ExitStack

import concourse.bass as bass
from concourse import mybir

ALU = mybir.AluOpType
ACT = mybir.ActivationFunctionType
AX = mybir.AxisListType
F32 = mybir.dt.float32
F32R = mybir.dt.float32r
BF16 = mybir.dt.bfloat16
U8 = mybir.dt.uint8

B, T, D = 16, 100, 512
S = 361
H, HD = 16, 32
C = D // 128
GH = 128 // HD
G = H // GH
KT = 3
KR = (S + KT - 1) // KT
SP = KT * KR
SE = S + S % 2
F = 2048
FC = F // 128
EPS = 1e-5
SCALE = HD ** -0.5
BIG = 3.3895313892515355e38
NS = 2 * B
MG = 4
NG = B // MG

T_AT = {0: 0, 1: 1, 3: 2, 4: 3}
XT_AT, Q_AT, QT_AT = 0, 2, 4
K_AT = {5: 0, 8: 1, 12: 2, 15: 3}
V_AT = {7: 0, 9: 1, 13: 2}
O_AT = 6
PV_AT = {7: 0, 11: 1, 15: 2, 3: 3}
LAG = 2
WORK = [("T", 0), ("T", 1), ("Q", 0), ("T", 2), ("T", 3), ("K", 0), ("V", 0), ("K", 1), ("V", 1),
        ("K", 2), ("V", 2), ("K", 3)]
assert all(h >= GH * g + GH - 1 for h, g in K_AT.items())
PARTS = 3


class Slot:

    def __init__(self, at, pair=None):
        self.at, self.odd = at, at % 2
        self.pair = at // 2 if pair is None else pair
        self.n = 2 * self.pair + self.odd
        self.layer = min(max(at // B, 0), 1)
        self.b = self.n - B * self.layer

    def step(self, k):
        at = self.at + k
        return Slot(at, self.pair + (self.at % 2 + k) // 2)

    @property
    def real(self):
        return 0 <= self.at < NS


def at_least(eng, sem, value):
    if not isinstance(value, int) or value > 0:
        eng.wait_ge(sem, value)


def slots(eng, body):
    for at in (-2, -1, 0):
        body(Slot(at))
    with eng.Fori(0, 6) as i:
        body(Slot(1, i))
        body(Slot(2, i + 1))
    for at in (13, 14, 15, 16):
        body(Slot(at))
    with eng.Fori(0, 6) as i:
        body(Slot(17, i + 8))
        body(Slot(18, i + 9))
    for at in (29, 30, 31, 32):
        body(Slot(at))


def row3(ap, b):
    return ap[bass.ds(b, 1), :, :].rearrange("o p d -> (o p) d")


def attention_layers(nc, a, hidden, ident, ident_ready):
    with ExitStack() as ctx:
        def sb(name, shape, dt=F32):
            return ctx.enter_context(nc.sbuf_tensor(name, shape, dt))

        def ps(name, shape):
            return ctx.enter_context(nc.psum_tensor(name, shape, F32))

        def sem(name):
            return ctx.enter_context(nc.semaphore(name))

        WN = ("q", "k", "v", "o")
        w_hi = {x: sb(f"w{x}_hi", [128, C, D], F32R) for x in WN}
        w_lo = {x: sb(f"w{x}_lo", [128, C, D], F32R) for x in WN}
        w_stage = sb("w_stage", [128, C, D])
        ctx_g, ctx_b = sb("ctx_g", [128, D]), sb("ctx_b", [128, D])
        ln1_g, ln1_b = sb("ln1_g", [T, D]), sb("ln1_b", [T, D])
        q_bias, o_bias = sb("q_bias", [T, D]), sb("o_bias", [T, D])
        k_bias, v_bias = sb("k_bias", [128, C]), sb("v_bias", [128, C])
        gate = sb("gate", [128, 1])
        ctx_in = sb("ctx_in", [KR, KT, D])
        x_in = sb("x_in", [T, D])
        ctx_st, ctx_mv = sb("ctx_st", [KR, KT, 6]), sb("ctx_mv", [KR, KT, 2])
        ctx_rs, ctx_nm = sb("ctx_rs", [KR, KT]), sb("ctx_nm", [KR, KT])
        x_st, x_mv, x_rs = sb("x_st", [T, 6]), sb("x_mv", [T, 2]), sb("x_rs", [T, 1])
        ctx_ve, x_ve = sb("ctx_ve", [KR, KT]), sb("x_ve", [T, 1])
        eps, minus_half = sb("eps", [128, 1]), sb("minus_half", [128, 1])
        cT_hi, cT_lo = sb("cT_hi", [128, C, SP + 1], F32R), sb("cT_lo", [128, C, SP + 1], F32R)
        xT_hi, xT_lo = sb("xT_hi", [128, C, T], F32R), sb("xT_lo", [128, C, T], F32R)
        q32 = sb("q32", [T, D])
        qT_hi, qT_lo = sb("qT_hi", [128, G, T], F32R), sb("qT_lo", [128, G, T], F32R)
        kT_hi, kT_lo = sb("kT_hi", [128, 2, SE], F32R), sb("kT_lo", [128, 2, SE], F32R)
        q_st = sb("q_st", [96, 2, GH, G, T], F32R)
        k_st = sb("k_st", [96, H, SE], F32R)
        v32 = sb("v32", [KR, 2, KT, D])
        mask8 = sb("mask8", [T, S], U8)
        minus_one, big = sb("minus_one", [T, 1]), sb("big", [T, 1])
        mask_add = sb("mask_add", [T, 2, S])
        p = sb("p", [T, 4, SP])
        p_min, p_sum, p_rec = sb("p_min", [T, 4]), sb("p_sum", [T, 4]), sb("p_rec", [T, 4])
        pT = sb("pT", [KR, 2, KT, GH, T])
        ao32 = sb("ao32", [128, G, T])
        ao_hi, ao_lo = sb("ao_hi", [128, G, T], F32R), sb("ao_lo", [128, G, T], F32R)
        res = sb("res", [T, D])
        x_out = sb("x_out", [T, D])

        work = ps("work", [128, 2, 512])
        side = ps("side", [128, 512])
        scores = ps("scores", [128, 2, 512])
        turned = ps("turned", [128, 2, 512])
        mixed = ps("mixed", [128, 512])

        consts_in, w_in = sem("consts_in"), sem("w_in")
        ctx_loaded, x_loaded, mask_loaded, res_loaded = (
            sem("ctx_loaded"), sem("x_loaded"), sem("mask_loaded"), sem("res_loaded"))
        q_stacked = sem("q_stacked")
        k_stacked = [sem(f"k_stacked{g}") for g in range(G)]
        x_stored = sem("x_stored")
        gate_done, w_hi_done = sem("gate_done"), sem("w_hi_done")
        ctx_scaled = sem("ctx_scaled")
        cT_hi_done, xT_hi_done, qT_hi_done, kT_hi_done = (
            sem("cT_hi_done"), sem("xT_hi_done"), sem("qT_hi_done"), sem("kT_hi_done"))
        v_done, exp_done, pT_done, ao_hi_done = (
            sem("v_done"), sem("exp_done"), sem("pT_done"), sem("ao_hi_done"))
        w_lo_done = sem("w_lo_done")
        ctx_stats, ctx_aggr, ctx_rstd, ctx_shift = (
            sem("ctx_stats"), sem("ctx_aggr"), sem("ctx_rstd"), sem("ctx_shift"))
        x_stats, x_aggr, x_rstd, x_scaled = (
            sem("x_stats"), sem("x_aggr"), sem("x_rstd"), sem("x_scaled"))
        cT_done, xT_done, q_done, qT_done, kT_done = (
            sem("cT_done"), sem("xT_done"), sem("q_done"), sem("qT_done"), sem("kT_done"))
        masked, rec_done, p_done = sem("masked"), sem("rec_done"), sem("p_done")
        ao32_done, ao_done, o_done = sem("ao32_done"), sem("ao_done"), sem("o_done")
        pads_done, mask_less_one, mask_lowest, mask_ready = (
            sem("pads_done"), sem("mask_less_one"), sem("mask_lowest"), sem("mask_ready"))
        ctx_var, x_var = sem("ctx_var"), sem("x_var")
        ctx_weighted, ctx_ready, x_weighted, x_ready, res_ready = (
            sem("ctx_weighted"), sem("ctx_ready"), sem("x_weighted"), sem("x_ready"),
            sem("res_ready"))
        cT_made, xT_made, q_made, qT_made, k_made, v_made, o_made = (
            sem("cT_made"), sem("xT_made"), sem("q_made"), sem("qT_made"), sem("k_made"),
            sem("v_made"), sem("o_made"))
        s_made, pT_made, pv_made = sem("s_made"), sem("pT_made"), sem("pv_made")

        block = ctx.enter_context(nc.Block())

        @block.sync
        def _(sp):
            for dst, src in ((ctx_g, a["g0"]), (ctx_b, a["b0"])):
                sp.dma_start(dst[:, :], src.rearrange("(o d) -> o d", o=1).broadcast_to([128, D])).then_inc(consts_in, 16)
            for dst, src in ((ln1_g, a["ln1_w"]), (ln1_b, a["ln1_b"]), (q_bias, a["q_b"]), (o_bias, a["cproj_b"])):
                sp.dma_start(dst[:, :], src.rearrange("(o d) -> o d", o=1).broadcast_to([T, D])).then_inc(consts_in, 16)
            for dst, src in ((k_bias, a["k_b"]), (v_bias, a["v_b"])):
                sp.dma_start(dst[:, :], src).then_inc(consts_in, 16)
            sp.dma_start(gate[:, :], a["gate"].rearrange("(o d) -> o d", o=1).broadcast_to([128, 1])).then_inc(consts_in, 16)

            def weights(layer, names):
                for x in names:
                    k = 4 * layer + WN.index(x)
                    at_least(sp, w_lo_done, k)
                    sp.dma_start(w_stage[:, :, :], a[f"w{layer}{x}"].rearrange("(c p) n -> p c n", p=128)).then_inc(w_in, 16)

            def body(s):
                n, m, z = s.step(1), s.step(2), s.step(-1)
                if s.at == 15:
                    weights(1, ("q", "k", "v"))
                if n.real:
                    at_least(sp, mask_ready, n.n)
                if m.real:
                    at_least(sp, cT_made, C * n.n + C)
                    sp.dma_start(ctx_in[:, :, :], a["ctx"][bass.ds(m.b, 1), :, :, :].rearrange("o k p d -> p (o k) d")).then_inc(ctx_loaded, 16)
                    at_least(sp, xT_made, n.n + 1)
                    if m.layer == 1:
                        at_least(sp, x_stored, 16 * (m.b + 1))
                    sp.dma_start(x_in[:, :], row3(a["x"] if m.layer == 0 else hidden, m.b)).then_inc(x_loaded, 16)
                if n.real:
                    sp.dma_start(mask8[:, :], a["mask"][bass.ds(n.b, 1), :].broadcast_to([T, S])).then_inc(mask_loaded, 16)
                if s.at == -2:
                    weights(0, WN)
                if n.real:
                    at_least(sp, qT_done, n.n + 1)
                    for part, src in enumerate((qT_hi, qT_lo, qT_hi)):
                        sp.dma_start(q_st[HD * part:HD * (part + 1), n.odd, :, :, :].bitcast(F32), src[:, :, :].bitcast(F32)).then_inc(q_stacked, 16)
                if z.real:
                    at_least(sp, o_done, z.n + 1)
                    sp.dma_start(row3(hidden, z.b), x_out[:, :]).then_inc(x_stored, 16)
                if s.at == 16:
                    weights(1, ("o",))
                if s.real:
                    at_least(sp, o_done, s.n)
                    sp.dma_start(res[:, :], row3(a["x"] if s.layer == 0 else hidden, s.b)).then_inc(res_loaded, 16)
                if n.real:
                    for g in range(G):
                        at_least(sp, kT_done, G * n.n + g + 1)
                        for part, src in enumerate((kT_hi, kT_hi, kT_lo)):
                            dst = k_st[HD * part:HD * (part + 1), GH * g:GH * (g + 1), :]
                            sp.dma_start(dst.bitcast(F32), src[:, g % 2, :].bitcast(F32)).then_inc(k_stacked[g], 16)

            slots(sp, body)
            sp.wait_ge(x_stored, 16 * NS)

        @block.gpsimd
        def _(pool):
            pool.memset(p[:, :, S:SP], 0.0).then_inc(pads_done, 1)
            pool.memset(minus_one[:, :], -1.0).then_inc(pads_done, 1)
            pool.memset(big[:, :], BIG).then_inc(pads_done, 1)
            pool.memset(eps[:, :], EPS).then_inc(pads_done, 1)
            pool.memset(minus_half[:, :], -0.5).then_inc(pads_done, 1)
            pool.wait_ge(pads_done, 5)

            def body(s):
                n, m, z = s.step(1), s.step(2), s.step(-1)
                if s.at == -2:
                    pool.wait_ge(consts_in, 16 * 9)
                if n.real:
                    pool.wait_ge(mask_loaded, 16 * (n.n + 1))
                    at_least(pool, masked, H * s.n)
                    half = mask_add[:, n.odd, :]
                    pool.tensor_tensor(half, mask8[:, :], minus_one[:, :].broadcast_to([T, S]), ALU.add).then_inc(mask_less_one, 1)
                    pool.wait_ge(mask_less_one, n.n + 1)
                    lowest = pool.tensor_tensor(half, half, big[:, :].broadcast_to([T, S]), ALU.mult)
                    lowest.then_inc(mask_lowest if n.layer == 0 else mask_ready, 1)
                    if n.layer == 0:
                        pool.wait_ge(mask_lowest, n.n + 1)
                        pool.tensor_tensor(half, half, half, ALU.add).then_inc(mask_ready, 1)
                if m.real and m.layer == 0:
                    pool.wait_ge(ctx_aggr, KT * (m.n + 1))
                    pool.tensor_tensor(ctx_ve[:, :], ctx_mv[:, :, 1], eps[0:KR, :].broadcast_to([KR, KT]), ALU.add).then_inc(ctx_var, 1)
                    pool.wait_ge(ctx_var, m.n + 1)
                    pool.tensor_tensor(ctx_rs[:, :], ctx_ve[:, :], minus_half[0:KR, :].broadcast_to([KR, KT]), ALU.pow).then_inc(ctx_rstd, 1)
                    pool.wait_ge(ctx_scaled, KT * (m.n + 1))
                    g3 = ctx_g[0:KR, :].unsqueeze(1).broadcast_to([KR, KT, D])
                    b3 = ctx_b[0:KR, :].unsqueeze(1).broadcast_to([KR, KT, D])
                    pool.tensor_tensor(ctx_in[:, :, :], ctx_in[:, :, :], g3, ALU.mult).then_inc(ctx_weighted, 1)
                    pool.wait_ge(ctx_weighted, m.n + 1)
                    pool.tensor_tensor(ctx_in[:, :, :], ctx_in[:, :, :], b3, ALU.add).then_inc(ctx_ready, 1)
                if m.real and m.layer == 1:
                    pool.wait_ge(x_aggr, m.b + 1)
                    pool.tensor_tensor(x_ve[:, :], x_mv[:, 1:2], eps[0:T, :], ALU.add).then_inc(x_var, 1)
                    pool.wait_ge(x_var, m.b + 1)
                    pool.tensor_tensor(x_rs[:, :], x_ve[:, :], minus_half[0:T, :], ALU.pow).then_inc(x_rstd, 1)
                    pool.wait_ge(x_scaled, m.b + 1)
                    pool.tensor_tensor(x_in[:, :], x_in[:, :], ln1_g[:, :], ALU.mult).then_inc(x_weighted, 1)
                    pool.wait_ge(x_weighted, m.b + 1)
                    pool.tensor_tensor(x_in[:, :], x_in[:, :], ln1_b[:, :], ALU.add).then_inc(x_ready, 1)
                if s.real and s.layer == 1:
                    pool.wait_ge(res_loaded, 16 * (s.n + 1))
                    pool.tensor_tensor(res[:, :], res[:, :], o_bias[:, :], ALU.add).then_inc(res_ready, 1)

            slots(pool, body)

        @block.scalar
        def _(act):
            act.wait_ge(consts_in, 16 * 9)
            act.activation(gate[:, :], gate[:, :], ACT.Tanh).then_inc(gate_done, 1)

            def split_weights(layer, names):
                for x in names:
                    k = 4 * layer + WN.index(x)
                    act.wait_ge(w_in, 16 * (k + 1))
                    if layer:
                        act.wait_ge({"q": q_made, "k": k_made, "v": v_made, "o": o_made}[x], B * {"q": 1, "k": G, "v": KT, "o": 1}[x])
                    act.copy(w_hi[x][:, :, :], w_stage[:, :, :]).then_inc(w_hi_done, 1)

            def context_affine(m):
                act.wait_ge(ctx_shift, m.n + 1)
                for k in range(KT):
                    act.activation(ctx_in[:, k, :], ctx_in[:, k, :], ACT.Identity, bias=ctx_nm[:, k:k + 1], scale=ctx_rs[:, k:k + 1]).then_inc(ctx_scaled, 1)

            def body(s):
                n, m, z = s.step(1), s.step(2), s.step(-1)
                if s.at == -2:
                    split_weights(0, WN)
                if s.at == 15:
                    split_weights(1, ("q", "k", "v"))
                for h in range(H):
                    if s.real:
                        act.wait_ge(masked, H * s.n + h + 1)
                        act.activation(p[:, h % 4, 0:S], p[:, h % 4, 0:S], ACT.Exp, bias=p_min[:, h % 4:h % 4 + 1], scale=-1.0,
                                       accum_out=p_sum[:, h % 4:h % 4 + 1]).then_inc(exp_done, 1)
                    if n.real:
                        if h == XT_AT:
                            act.wait_ge(xT_made, n.n + 1)
                            at_least(act, q_made, n.n)
                            act.copy(xT_hi[:, :, :], side[:, 0:C * T].rearrange("p (c t) -> p c t", c=C)).then_inc(xT_hi_done, 1)
                        if h in T_AT:
                            c = T_AT[h]
                            act.wait_ge(cT_made, C * n.n + c + 1)
                            at_least(act, k_made, G * n.n)
                            act.copy(cT_hi[:, c, 0:SP], work[:, WORK.index(("T", c)) % 2, 0:SP]).then_inc(cT_hi_done, 1)
                        if h == QT_AT:
                            act.wait_ge(qT_made, n.n + 1)
                            at_least(act, q_stacked, 16 * PARTS * n.n)
                            act.copy(qT_hi[:, :, :], side[:, 0:G * T].rearrange("p (c t) -> p c t", c=G)).then_inc(qT_hi_done, 1)
                        if h in K_AT:
                            g = K_AT[h]
                            act.wait_ge(k_made, G * n.n + g + 1)
                            at_least(act, k_stacked[(g + 2) % G], 16 * PARTS * (n.n + g // 2))
                            src = work[:, WORK.index(("K", g)) % 2, 0:SE]
                            if n.layer == 0:
                                act.copy(kT_hi[:, g % 2, :], src).then_inc(kT_hi_done, 1)
                            else:
                                act.activation(kT_hi[:, g % 2, :], src, ACT.Identity, bias=k_bias[:, g:g + 1]).then_inc(kT_hi_done, 1)
                        if h in V_AT:
                            k = V_AT[h]
                            act.wait_ge(v_made, KT * n.n + k + 1)
                            at_least(act, pv_made, G * s.n)
                            act.copy(v32[:, n.odd, k, :], work[0:KR, WORK.index(("V", k)) % 2, :]).then_inc(v_done, 1)
                    y, hh = (s, h - LAG) if h >= LAG else (z, h - LAG + H)
                    if y.real:
                        act.wait_ge(pT_made, H * y.n + hh + 1)
                        g, j = hh // GH, hh % GH
                        if j == 0:
                            at_least(act, pv_made, G * y.n + g - 1)
                        act.copy(pT[:, g % 2, :, j, :], turned[0:KR, hh % 2, 0:KT * T].rearrange("p (k t) -> p k t", k=KT)).then_inc(pT_done, 1)
                    if z.real and h == 4:
                        act.wait_ge(ao32_done, z.n + 1)
                        at_least(act, o_made, z.n)
                        act.copy(ao_hi[:, :, :], ao32[:, :, :]).then_inc(ao_hi_done, 1)
                    if m.real and m.layer == 0 and h == 12:
                        context_affine(m)
                    if s.at == 16 and h == 8:
                        split_weights(1, ("o",))
                    if s.at == NS and h == 6:
                        break

            slots(act, body)

        @block.vector
        def _(dve):
            dve.wait_ge(gate_done, 1)
            dve.wait_ge(pads_done, 5)

            def split_weights(layer, names):
                for x in names:
                    k = 4 * layer + WN.index(x)
                    dve.wait_ge(w_hi_done, k + 1)
                    dve.tensor_tensor(w_lo[x][:, :, :], w_stage[:, :, :], w_hi[x][:, :, :].bitcast(F32), ALU.subtract).then_inc(w_lo_done, 1)

            def body(s):
                n, m, z = s.step(1), s.step(2), s.step(-1)
                if s.at == -2:
                    split_weights(0, WN)
                if s.at == 15:
                    split_weights(1, ("q", "k", "v"))

                for h in range(H):
                    y, hh = (s, h - 1) if h else (z, H - 1)
                    if s.real:
                        if h == 0:
                            dve.wait_ge(mask_ready, s.n + 1)
                        dve.wait_ge(s_made, H * s.n + h + 1)
                        at_least(dve, pT_made, H * s.n + h - 3)
                    if m.real and h == 10:
                        if m.layer == 0:
                            dve.wait_ge(ctx_stats, KT * (m.n + 1))
                        else:
                            dve.wait_ge(x_stats, m.b + 1)
                    if y.real:
                        dve.wait_ge(exp_done, H * y.n + hh + 1)
                        dve.reciprocal(p_rec[:, hh % 4:hh % 4 + 1], p_sum[:, hh % 4:hh % 4 + 1]).then_inc(rec_done, 1)
                    if s.real:
                        dve.tensor_tensor_reduce(out=p[:, h % 4, 0:S], in0=scores[0:T, h % 2, 0:S], in1=mask_add[:, s.odd, :],
                                                 scale=-SCALE, scalar=BIG, op0=ALU.add, op1=ALU.min,
                                                 accum_out=p_min[:, h % 4:h % 4 + 1]).then_inc(masked, 1)
                    if y.real:
                        dve.wait_ge(rec_done, H * y.n + hh + 1)
                        dve.tensor_scalar(p[:, hh % 4, 0:S], p[:, hh % 4, 0:S], p_rec[:, hh % 4:hh % 4 + 1], None, ALU.mult).then_inc(p_done, 1)
                    if n.real:
                        if h == XT_AT:
                            dve.wait_ge(xT_hi_done, n.n + 1)
                            dve.tensor_tensor(xT_lo[:, :, :], side[:, 0:C * T].rearrange("p (c t) -> p c t", c=C), xT_hi[:, :, :].bitcast(F32), ALU.subtract).then_inc(xT_done, 1)
                        if h in T_AT:
                            c = T_AT[h]
                            dve.wait_ge(cT_hi_done, C * n.n + c + 1)
                            dve.tensor_tensor(cT_lo[:, c, 0:SP], work[:, WORK.index(("T", c)) % 2, 0:SP], cT_hi[:, c, 0:SP].bitcast(F32), ALU.subtract).then_inc(cT_done, 1)
                        if h == Q_AT:
                            dve.wait_ge(q_made, n.n + 1)
                            at_least(dve, qT_made, n.n)
                            src = work[0:T, WORK.index(("Q", 0)) % 2, :]
                            if n.layer == 0:
                                dve.tensor_copy(q32[:, :], src).then_inc(q_done, 1)
                            else:
                                dve.tensor_tensor(q32[:, :], src, q_bias[:, :], ALU.add).then_inc(q_done, 1)
                        if h == QT_AT:
                            dve.wait_ge(qT_hi_done, n.n + 1)
                            dve.tensor_tensor(qT_lo[:, :, :], side[:, 0:G * T].rearrange("p (c t) -> p c t", c=G), qT_hi[:, :, :].bitcast(F32), ALU.subtract).then_inc(qT_done, 1)
                        if h in K_AT:
                            g = K_AT[h]
                            dve.wait_ge(kT_hi_done, G * n.n + g + 1)
                            src = work[:, WORK.index(("K", g)) % 2, 0:SE]
                            hi = kT_hi[:, g % 2, :].bitcast(F32)
                            if n.layer == 0:
                                dve.tensor_tensor(kT_lo[:, g % 2, :], src, hi, ALU.subtract).then_inc(kT_done, 1)
                            else:
                                dve.scalar_tensor_tensor(kT_lo[:, g % 2, :], src, k_bias[:, g:g + 1], hi, ALU.add, ALU.subtract).then_inc(kT_done, 1)
                    if z.real and h == 4:
                        dve.wait_ge(pv_made, G * z.n + G)
                        src = mixed[:, 0:G * T].rearrange("p (g t) -> p g t", g=G)
                        if z.layer == 0:
                            dve.tensor_copy(ao32[:, :, :], src).then_inc(ao32_done, 1)
                        else:
                            dve.tensor_tensor(ao32[:, :, :], src, v_bias[:, :].unsqueeze(2).broadcast_to([128, G, T]), ALU.add).then_inc(ao32_done, 1)
                    if z.real and h == 5:
                        dve.wait_ge(ao_hi_done, z.n + 1)
                        dve.tensor_tensor(ao_lo[:, :, :], ao32[:, :, :], ao_hi[:, :, :].bitcast(F32), ALU.subtract).then_inc(ao_done, 1)
                    if z.real and h == O_AT:
                        dve.wait_ge(o_made, z.n + 1)
                        at_least(dve, x_stored, 16 * z.n)
                        if z.layer == 0:
                            dve.wait_ge(res_loaded, 16 * (z.n + 1))
                            dve.scalar_tensor_tensor(x_out[:, :], side[0:T, :], gate[0:T, :], res[:, :], ALU.mult, ALU.add).then_inc(o_done, 1)
                        else:
                            dve.wait_ge(res_ready, z.b + 1)
                            dve.tensor_tensor(x_out[:, :], side[0:T, :], res[:, :], ALU.add).then_inc(o_done, 1)
                    if m.real and m.layer == 0 and h in (7, 8, 9):
                        k = h - 7
                        dve.wait_ge(ctx_loaded, 16 * (m.n + 1))
                        dve.bn_stats(ctx_st[:, k, :], ctx_in[:, k, :]).then_inc(ctx_stats, 1)
                    if m.real and m.layer == 0 and h == 10:
                        for k in range(KT):
                            dve.bn_aggr(ctx_mv[:, k, :], ctx_st[:, k, :]).then_inc(ctx_aggr, 1)
                    if m.real and m.layer == 0 and h == 11:
                        dve.wait_ge(ctx_rstd, m.n + 1)
                        dve.scalar_tensor_tensor(ctx_nm[:, :], ctx_mv[:, :, 0], -1.0, ctx_rs[:, :], ALU.mult, ALU.mult).then_inc(ctx_shift, 1)
                    if m.real and m.layer == 1 and h == 9:
                        dve.wait_ge(x_loaded, 16 * (m.n + 1))
                        dve.bn_stats(x_st[:, :], x_in[:, :]).then_inc(x_stats, 1)
                    if m.real and m.layer == 1 and h == 10:
                        dve.bn_aggr(x_mv[:, :], x_st[:, :]).then_inc(x_aggr, 1)
                    if m.real and m.layer == 1 and h == 11:
                        dve.wait_ge(x_rstd, m.b + 1)
                        dve.tensor_scalar(x_in[:, :], x_in[:, :], x_mv[:, 0:1], x_rs[:, 0:1], ALU.subtract, ALU.mult).then_inc(x_scaled, 1)
                    if s.at == 16 and h == 8:
                        split_weights(1, ("o",))

            slots(dve, body)

        @block.tensor
        def _(pe):
            pe.wait_ge(ident_ready, 2)

            def three(out, pairs):
                todo = [(x, y) for (x_hi, x_lo, y_hi, y_lo) in pairs for (x, y) in ((x_hi, y_hi), (x_hi, y_lo), (x_lo, y_hi))]
                for i, (x, y) in enumerate(todo):
                    last = pe.matmul(out, x, y, start=i == 0, stop=i == len(todo) - 1)
                return last

            def work_bank(item, n):
                at = WORK.index(item)
                kind, i = WORK[at - 2]
                slot = n if at >= 2 else n.step(-1)
                done, per = {"T": (cT_done, C), "K": (kT_done, G), "V": (v_done, KT), "Q": (q_done, 1)}[kind]
                at_least(pe, done, per * slot.n + i + 1)
                return work[:, at % 2, :]

            def body(s):
                n, z = s.step(1), s.step(-1)
                for h in range(H):
                    if s.real:
                        if h == 0:
                            pe.wait_ge(q_stacked, 16 * PARTS * (s.n + 1))
                        if h % GH == 0:
                            pe.wait_ge(k_stacked[h // GH], 16 * PARTS * (s.n + 1))
                        at_least(pe, masked, H * s.n + h - 1)
                        pe.matmul(scores[0:T, h % 2, 0:SE], q_st[:, s.odd, h % GH, h // GH, :], k_st[:, h, :], start=True, stop=True).then_inc(s_made, 1)
                    if n.real:
                        if h == XT_AT:
                            if n.layer == 0:
                                pe.wait_ge(x_loaded, 16 * (n.n + 1))
                            else:
                                pe.wait_ge(x_ready, n.b + 1)
                            at_least(pe, o_done, n.n - 2)
                            for c in range(C):
                                last = pe.transpose(side[:, c * T:(c + 1) * T], x_in[:, c * 128:(c + 1) * 128], ident[0:T, 0:T])
                            last.then_inc(xT_made, 1)
                        if h in T_AT:
                            c = T_AT[h]
                            bank = work_bank(("T", c), n)
                            if c == 0:
                                if n.layer == 0:
                                    pe.wait_ge(ctx_ready, n.n + 1)
                                else:
                                    pe.wait_ge(ctx_loaded, 16 * (n.n + 1))
                            for k in range(KT):
                                last = pe.transpose(bank[:, k * KR:(k + 1) * KR], ctx_in[:, k, c * 128:(c + 1) * 128], ident[0:KR, 0:KR])
                            last.then_inc(cT_made, 1)
                        if h == Q_AT:
                            bank = work_bank(("Q", 0), n)
                            pe.wait_ge(xT_done, n.n + 1)
                            pe.wait_ge(w_lo_done, 4 * n.layer + 1)
                            three(bank[0:T, :], [(xT_hi[:, c, :], xT_lo[:, c, :], w_hi["q"][:, c, :], w_lo["q"][:, c, :]) for c in range(C)]).then_inc(q_made, 1)
                        if h == QT_AT:
                            pe.wait_ge(q_done, n.n + 1)
                            pe.wait_ge(xT_done, n.n + 1)
                            for g in range(G):
                                last = pe.transpose(side[:, g * T:(g + 1) * T], q32[:, g * 128:(g + 1) * 128], ident[0:T, 0:T])
                            last.then_inc(qT_made, 1)
                        if h in K_AT:
                            g = K_AT[h]
                            bank = work_bank(("K", g), n)
                            pe.wait_ge(cT_done, C * n.n + C)
                            pe.wait_ge(w_lo_done, 4 * n.layer + 2)
                            w = slice(g * 128, (g + 1) * 128)
                            three(bank[:, 0:SE], [(w_hi["k"][:, c, w], w_lo["k"][:, c, w], cT_hi[:, c, 0:SE], cT_lo[:, c, 0:SE]) for c in range(C)]).then_inc(k_made, 1)
                        if h in V_AT:
                            k = V_AT[h]
                            bank = work_bank(("V", k), n)
                            pe.wait_ge(w_lo_done, 4 * n.layer + 3)
                            r = slice(k * KR, (k + 1) * KR)
                            three(bank[0:KR, :], [(cT_hi[:, c, r], cT_lo[:, c, r], w_hi["v"][:, c, :], w_lo["v"][:, c, :]) for c in range(C)]).then_inc(v_made, 1)
                    if z.real and h == O_AT:
                        pe.wait_ge(ao_done, z.n + 1)
                        if z.n is not None and z.layer == 1:
                            pe.wait_ge(w_lo_done, 8)
                        else:
                            pe.wait_ge(w_lo_done, 4)
                        if n.real:
                            pe.wait_ge(qT_done, n.n + 1)
                        elif z.at >= 1:
                            pe.wait_ge(o_done, z.n)
                        three(side[0:T, :], [(ao_hi[:, c, :], ao_lo[:, c, :], w_hi["o"][:, c, :], w_lo["o"][:, c, :]) for c in range(C)]).then_inc(o_made, 1)
                    y, hh = (s, h - LAG) if h >= LAG else (z, h - LAG + H)
                    if y.real:
                        pe.wait_ge(p_done, H * y.n + hh + 1)
                        at_least(pe, pT_done, H * y.n + hh - 1)
                        for k in range(KT):
                            last = pe.transpose(turned[0:KR, hh % 2, k * T:(k + 1) * T], p[:, hh % 4, k * KR:(k + 1) * KR], ident[0:T, 0:T])
                        last.then_inc(pT_made, 1)
                    if h in PV_AT:
                        g = PV_AT[h]
                        y = z if g == G - 1 else s
                        if y.real:
                            pe.wait_ge(pT_done, H * y.n + GH * (g + 1))
                            if g == 0:
                                pe.wait_ge(v_done, KT * (y.n + 1))
                                at_least(pe, ao32_done, y.n)
                            for k in range(KT):
                                for j in range(GH):
                                    hd = (GH * g + j) * HD
                                    last = pe.matmul(mixed[32 * j:32 * j + 32, g * T:(g + 1) * T], v32[:, y.odd, k, hd:hd + HD], pT[:, g % 2, k, j, :],
                                                     start=k == 0, stop=k == KT - 1)
                            last.then_inc(pv_made, 1)
                    if s.at == NS and h == O_AT:
                        break

            slots(pe, body)


def mlp(nc, a, hidden, out, ident):
    with ExitStack() as ctx:
        def sb(name, shape, dt=F32):
            return ctx.enter_context(nc.sbuf_tensor(name, shape, dt))

        def sem(name):
            return ctx.enter_context(nc.semaphore(name))

        WP = 2 * C
        N = MG * T
        wf_hi, wf_lo = sb("wf_hi", [128, C, F], F32R), sb("wf_lo", [128, C, F], F32R)
        wp_hi, wp_lo = sb("wp_hi", [128, FC, D], F32R), sb("wp_lo", [128, FC, D], F32R)
        stage = sb("stage", [128, 2, F])
        ln2_g, ln2_b, p_bias = sb("ln2_g", [T, D]), sb("ln2_b", [T, D]), sb("p_bias", [T, D])
        f_bias = sb("f_bias", [128, FC])
        x2, y = sb("x2", [T, MG, D]), sb("y", [T, MG, D])
        st, mv, rs = sb("st", [T, MG, 6]), sb("mv", [T, MG, 2]), sb("rs", [T, MG])
        after_stats = sb("after_stats", [T, 1])
        ve, eps, minus_half = sb("ve", [T, MG]), sb("mlp_eps", [T, 1]), sb("mlp_minus_half", [T, 1])
        yT_hi, yT_lo = sb("yT_hi", [128, C, N], F32R), sb("yT_lo", [128, C, N], F32R)
        h32 = sb("h32", [128, 2, N])
        h_hi, h_lo = sb("h_hi", [128, 2, N], F32R), sb("h_lo", [128, 2, N], F32R)
        turned = ctx.enter_context(nc.psum_tensor("mlp_turned", [128, 2, 512], F32))
        up = ctx.enter_context(nc.psum_tensor("mlp_up", [128, 2, 512], F32))
        down = ctx.enter_context(nc.psum_tensor("mlp_down", [128, MG, 512], F32))

        consts_in, w_in0, w_in1, x_in, stored = (
            sem("mlp_consts_in"), sem("mlp_w_in0"), sem("mlp_w_in1"), sem("mlp_x_in"), sem("stored"))
        w_in = (w_in0, w_in1)
        w_hi_done, w_lo_done = sem("mlp_w_hi_done"), sem("mlp_w_lo_done")
        stats_done, aggr_done, rstd_done, scaled, weighted, y_ready, res_ready = (
            sem("mlp_stats"), sem("mlp_aggr"), sem("mlp_rstd"), sem("mlp_scaled"), sem("mlp_weighted"),
            sem("mlp_y_ready"), sem("mlp_res_ready"))
        pads_done, var_done = sem("mlp_pads_done"), sem("mlp_var_done")
        yT_made, yT_hi_done, yT_done = sem("yT_made"), sem("yT_hi_done"), sem("yT_done")
        up_made, gelu_done, h_hi_done, h_done, down_made, out_done = (
            sem("up_made"), sem("gelu_done"), sem("h_hi_done"), sem("h_done"), sem("down_made"), sem("out_done"))

        block = ctx.enter_context(nc.Block())

        def groups(eng, body):
            body(-1)
            body(0, True)
            with eng.Fori(1, NG - 1) as i:
                body(i, True)
            body(NG - 1)

        @block.sync
        def _(sp):
            hid = hidden.rearrange("(g m) t d -> g t m d", m=MG)
            dst = out.rearrange("(g m) t d -> g t m d", m=MG)

            def load(g):
                at_least(sp, stored, 16 * g)
                sp.dma_start(x2[:, :, :], hid[bass.ds(g, 1), :, :, :].rearrange("o t m d -> t (o m) d")).then_inc(x_in, 16)

            for dstv, src in ((ln2_g, a["ln2_w"]), (ln2_b, a["ln2_b"]), (p_bias, a["proj_b"])):
                sp.dma_start(dstv[:, :], src.rearrange("(o d) -> o d", o=1).broadcast_to([T, D])).then_inc(consts_in, 16)
            sp.dma_start(f_bias[:, :], a["fc_b"]).then_inc(consts_in, 16)
            load(0)
            fc = a["fc_w"].rearrange("(c p) n -> c p n", p=128)
            pr = a["proj_w"].rearrange("(k c p) n -> k p c n", p=128, k=C)
            for k in range(WP):
                at_least(sp, w_lo_done, k - 1)
                src = fc[k, :, :] if k < C else pr[k - C, :, :, :]
                d = stage[:, k % 2, :] if k < C else stage[:, k % 2, :].rearrange("p (c n) -> p c n", n=D)
                sp.dma_start(d, src).then_inc(w_in[k % 2], 16)

            def body(g, more=False):
                if isinstance(g, int) and g < 0:
                    return
                sp.wait_ge(out_done, MG * (g + 1))
                sp.dma_start(dst[bass.ds(g, 1), :, :, :].rearrange("o t m d -> t (o m) d"), x2[:, :, :]).then_inc(stored, 16)
                if more:
                    load(g + 1)

            groups(sp, body)
            sp.wait_ge(stored, 16 * NG)

        @block.gpsimd
        def _(pool):
            pool.wait_ge(consts_in, 16 * 4)
            pool.memset(eps[:, :], EPS).then_inc(pads_done, 1)
            pool.memset(minus_half[:, :], -0.5).then_inc(pads_done, 1)
            pool.wait_ge(pads_done, 2)

            def prepare(g):
                pool.wait_ge(aggr_done, MG * (g + 1))
                pool.tensor_tensor(ve[:, :], mv[:, :, 1], eps[:, :].broadcast_to([T, MG]), ALU.add).then_inc(var_done, 1)
                pool.wait_ge(var_done, g + 1)
                pool.tensor_tensor(rs[:, :], ve[:, :], minus_half[:, :].broadcast_to([T, MG]), ALU.pow).then_inc(rstd_done, 1)
                for i in range(MG):
                    pool.wait_ge(scaled, MG * g + i + 1)
                    pool.tensor_tensor(y[:, i, :], y[:, i, :], ln2_g[:, :], ALU.mult).then_inc(weighted, 1)
                    pool.wait_ge(weighted, MG * g + i + 1)
                    pool.tensor_tensor(y[:, i, :], y[:, i, :], ln2_b[:, :], ALU.add).then_inc(y_ready, 1)
                for i in range(MG):
                    pool.tensor_tensor(x2[:, i, :], x2[:, i, :], p_bias[:, :], ALU.add).then_inc(res_ready, 1)

            def body(g, more=False):
                if more or (isinstance(g, int) and g < 0):
                    prepare(g + 1)

            groups(pool, body)

        @block.scalar
        def _(act):
            act.wait_ge(consts_in, 16 * 4)
            for k in range(WP):
                act.wait_ge(w_in[k % 2], 16 * (k // 2 + 1))
                d = wf_hi[:, k, :] if k < C else wp_hi[:, C * (k - C):C * (k - C + 1), :]
                s = stage[:, k % 2, :] if k < C else stage[:, k % 2, :].rearrange("p (c n) -> p c n", n=D)
                act.copy(d, s).then_inc(w_hi_done, 1)

            def body(g, more=False):
                if isinstance(g, int) and g < 0:
                    return
                for c in range(C):
                    act.wait_ge(yT_made, C * g + c + 1)
                    at_least(act, up_made, FC * g)
                    act.copy(yT_hi[:, c, :], turned[:, c % 2, 0:N]).then_inc(yT_hi_done, 1)
                for k in range(FC):
                    act.wait_ge(up_made, FC * g + k + 1)
                    at_least(act, h_done, FC * g + k - 1)
                    act.activation(h32[:, k % 2, :], up[:, k % 2, 0:N], ACT.Gelu_apprx_tanh, bias=f_bias[:, k:k + 1]).then_inc(gelu_done, 1)
                    act.wait_ge(gelu_done, FC * g + k + 1)
                    at_least(act, down_made, FC * g + k - 1)
                    act.copy(h_hi[:, k % 2, :], h32[:, k % 2, :]).then_inc(h_hi_done, 1)

            groups(act, body)

        @block.vector
        def _(dve):
            def normalise(g):
                dve.wait_ge(x_in, 16 * (g + 1))
                for i in range(MG):
                    dve.bn_stats(st[:, i, :], x2[:, i, :]).then_inc(stats_done, 1)
                dve.wait_ge(stats_done, MG * (g + 1))
                dve.memset(after_stats[:, :], 0.0)
                for i in range(MG):
                    dve.bn_aggr(mv[:, i, :], st[:, i, :]).then_inc(aggr_done, 1)
                dve.wait_ge(rstd_done, g + 1)
                at_least(dve, yT_made, C * g)
                for i in range(MG):
                    dve.tensor_scalar(y[:, i, :], x2[:, i, :], mv[:, i, 0:1], rs[:, i:i + 1], ALU.subtract, ALU.mult).then_inc(scaled, 1)

            def split_weights(ks):
                for k in ks:
                    dve.wait_ge(w_hi_done, k + 1)
                    if k < C:
                        dve.tensor_tensor(wf_lo[:, k, :], stage[:, k % 2, :], wf_hi[:, k, :].bitcast(F32), ALU.subtract).then_inc(w_lo_done, 1)
                    else:
                        c = slice(C * (k - C), C * (k - C + 1))
                        dve.tensor_tensor(wp_lo[:, c, :], stage[:, k % 2, :].rearrange("p (c n) -> p c n", n=D), wp_hi[:, c, :].bitcast(F32), ALU.subtract).then_inc(w_lo_done, 1)

            def body(g, more=False):
                if isinstance(g, int) and g < 0:
                    normalise(0)
                    split_weights(range(WP))
                    return
                for c in range(C):
                    dve.wait_ge(yT_hi_done, C * g + c + 1)
                    dve.tensor_tensor(yT_lo[:, c, :], turned[:, c % 2, 0:N], yT_hi[:, c, :].bitcast(F32), ALU.subtract).then_inc(yT_done, 1)
                for k in range(FC):
                    dve.wait_ge(h_hi_done, FC * g + k + 1)
                    dve.tensor_tensor(h_lo[:, k % 2, :], h32[:, k % 2, :], h_hi[:, k % 2, :].bitcast(F32), ALU.subtract).then_inc(h_done, 1)
                dve.wait_ge(down_made, FC * (g + 1))
                dve.wait_ge(res_ready, MG * (g + 1))
                for i in range(MG):
                    dve.tensor_tensor(x2[:, i, :], down[0:T, i, :], x2[:, i, :], ALU.add).then_inc(out_done, 1)
                if more:
                    normalise(g + 1)

            groups(dve, body)

        @block.tensor
        def _(pe):
            def body(g, more=False):
                if isinstance(g, int) and g < 0:
                    return
                for c in range(C):
                    if c == 0:
                        pe.wait_ge(y_ready, MG * (g + 1))
                    if c >= 2:
                        pe.wait_ge(yT_done, C * g + c - 1)
                    else:
                        at_least(pe, yT_done, C * g)
                    for i in range(MG):
                        last = pe.transpose(turned[:, c % 2, i * T:(i + 1) * T], y[:, i, c * 128:(c + 1) * 128], ident[0:T, 0:T])
                    last.then_inc(yT_made, 1)
                for k in range(FC + 1):
                    if k < FC:
                        if k == 0:
                            pe.wait_ge(yT_done, C * (g + 1))
                            pe.wait_ge(w_lo_done, C)
                        at_least(pe, gelu_done, FC * g + k - 1)
                        f = slice(k * 128, (k + 1) * 128)
                        todo = [xy for c in range(C) for xy in ((wf_hi[:, c, f], yT_hi[:, c, :]), (wf_hi[:, c, f], yT_lo[:, c, :]), (wf_lo[:, c, f], yT_hi[:, c, :]))]
                        for i, (w, v) in enumerate(todo):
                            last = pe.matmul(up[:, k % 2, 0:N], w, v, start=i == 0, stop=i == len(todo) - 1)
                        last.then_inc(up_made, 1)
                    if k >= 1:
                        j = k - 1
                        pe.wait_ge(h_done, FC * g + j + 1)
                        if j == 0:
                            at_least(pe, out_done, MG * g)
                        if j % C == 0:
                            pe.wait_ge(w_lo_done, C + j // C + 1)
                        for i in range(MG):
                            t = slice(i * T, (i + 1) * T)
                            for e, (v, w) in enumerate(((h_hi[:, j % 2, t], wp_hi[:, j, :]), (h_hi[:, j % 2, t], wp_lo[:, j, :]), (h_lo[:, j % 2, t], wp_hi[:, j, :]))):
                                last = pe.matmul(down[0:T, i, :], v, w, start=j == 0 and e == 0, stop=j == FC - 1 and e == 2)
                        last.then_inc(down_made, 1)

            groups(pe, body)


def build(nc, a, out):
    hidden = nc.dram_tensor("hidden", [B, T, D], F32, kind="Internal").ap()
    with ExitStack() as ctx:
        ident = ctx.enter_context(nc.sbuf_tensor("ident", [128, 128], F32))
        ident_ready = ctx.enter_context(nc.semaphore("ident_ready"))
        with nc.Block() as block:
            @block.gpsimd
            def _(pool):
                pool.memset(ident[:, :], 0.0).then_inc(ident_ready, 1)
                pool.wait_ge(ident_ready, 1)
                pool.affine_select(out=ident[:, :], in_=ident[:, :], compare_op=ALU.not_equal, fill=1.0, base=0,
                                   pattern=[[-1, 128]], channel_multiplier=1).then_inc(ident_ready, 1)
        attention_layers(nc, a, hidden, ident, ident_ready)
        mlp(nc, a, hidden, out, ident)


def kernel(x, ctx_2048, mask_BxS2_bf1, **w):
    import numpy as np
    import concourse.bacc as bacc
    from concourse.bass_utils import run_bass_kernel_spmd

    ctx = np.zeros((B, SP, D), np.float32)
    ctx[:, :S, :] = np.asarray(ctx_2048)
    l0, l1 = "L0_xattn_", "L1_xattn_"

    def columns(v):
        return np.asarray(v).reshape(-1, 128).T

    def by_dim(v):
        v = np.asarray(v)
        return v.reshape(-1, G, GH, HD).transpose(0, 1, 3, 2).reshape(v.shape)

    named = {
        "x": x, "ctx": ctx.reshape(B, KT, KR, D), "mask": np.asarray(mask_BxS2_bf1).view(np.uint8),
        "w0q": by_dim(np.asarray(w[l0 + "Wq"]).T), "w0k": by_dim(np.asarray(w[l0 + "Wk"]).T), "w0v": np.asarray(w[l0 + "Wv"]).T,
        "w0o": np.asarray(w[l0 + "Wo"]).T, "g0": w[l0 + "ln_gamma"], "b0": w[l0 + "ln_beta"], "gate": w[l0 + "gate"],
        "w1q": by_dim(w[l1 + "q_w"]), "w1k": by_dim(w[l1 + "k_w"]), "w1v": w[l1 + "v_w"], "w1o": w[l1 + "cproj_w"],
        "ln1_w": w[l1 + "ln1_w"], "ln1_b": w[l1 + "ln1_b"], "q_b": by_dim(w[l1 + "q_b"]), "k_b": columns(by_dim(w[l1 + "k_b"])), "v_b": columns(w[l1 + "v_b"]),
        "cproj_b": w[l1 + "cproj_b"], "ln2_w": w[l1 + "ln2_w"], "ln2_b": w[l1 + "ln2_b"], "fc_w": w[l1 + "fc_w"],
        "fc_b": columns(w[l1 + "fc_b"]), "proj_w": w[l1 + "proj_w"], "proj_b": w[l1 + "proj_b"],
    }
    nc = bacc.Bacc("TRN2", target_bir_lowering=False, num_devices=1)
    arrays, a = {}, {}
    for name, value in named.items():
        value = np.ascontiguousarray(value)
        arrays[f"in_{name}"] = value
        a[name] = nc.dram_tensor(f"in_{name}", value.shape, mybir.dt.from_np(value.dtype), kind="ExternalInput").ap()
    out = nc.dram_tensor("out", [B, T, D], F32, kind="ExternalOutput").ap()
    build(nc, a, out)
    r = run_bass_kernel_spmd(nc, [arrays], core_ids=[0])
    return r.results[0]["out"]
```

```python
from contextlib import ExitStack

import concourse.bass as bass
from concourse import mybir

ALU = mybir.AluOpType
ACT = mybir.ActivationFunctionType
AX = mybir.AxisListType
F32 = mybir.dt.float32
F32R = mybir.dt.float32r
BF16 = mybir.dt.bfloat16
U8 = mybir.dt.uint8

B, T, D = 16, 100, 512
S = 361
H, HD = 16, 32
C = D // 128
GH = 128 // HD
G = H // GH
KT = 3
KR = (S + KT - 1) // KT
SP = KT * KR
SE = S + S % 2
F = 2048
FC = F // 128
EPS = 1e-5
SCALE = HD ** -0.5
BIG = 3.3895313892515355e38
NS = 2 * B
MG = 4
NG = B // MG

XT_AT, T_AT, QT_AT = 0, {3: 0, 4: 1, 5: 2, 6: 3}, 7
WORK = (("K", 3, 0, {0: 12}), ("V", 2, 0, {1: 8, 2: 4}), ("Q", 0, 1, {3: 6, 4: 6}), ("O", 0, -1, {5: 6, 6: 6}),
        ("V", 0, 1, {8: 8, 9: 4}), ("K", 0, 1, {9: 6, 10: 6}), ("K", 1, 1, {10: 6, 11: 2, 12: 4}),
        ("K", 2, 1, {12: 8, 13: 4}), ("V", 1, 1, {13: 5, 14: 7}))
assert all(sum(steps.values()) == 3 * C for _, _, _, steps in WORK)
O_END = next(max(steps) for kind, _, _, steps in WORK if kind == "O")
PV_AT = {7: 0, 11: 1, 15: 2, 2: 3}
AO_AT = 2
LAG = 2
CTX_STATS_AT, CTX_AGGR_AT, CTX_SHIFT_AT = {10: 0, 11: 1, 12: 2}, 13, 14
X_STATS_AT, X_AGGR_AT, X_SCALE_AT = 8, 9, 10
WN = ("q", "k", "v", "o")
SPLIT_AT = {(-1, 1): (0, "q"), (-1, 6): (0, "k"), (-1, 7): (0, "v"), (-1, 12): (0, "o"),
            (14, 6): (1, "q"), (15, 1): (1, "k"), (15, 6): (1, "v"), (16, 8): (1, "o")}
PARTS = 3


class Slot:

    def __init__(self, at, pair=None):
        self.at, self.odd = at, at % 2
        self.pair = at // 2 if pair is None else pair
        self.n = 2 * self.pair + self.odd
        self.layer = min(max(at // B, 0), 1)
        self.b = self.n - B * self.layer

    def step(self, k):
        at = self.at + k
        return Slot(at, self.pair + (self.at % 2 + k) // 2)

    @property
    def real(self):
        return 0 <= self.at < NS


def at_least(eng, sem, value):
    if not isinstance(value, int) or value > 0:
        eng.wait_ge(sem, value)


def slots(eng, body):
    for at in (-2, -1, 0):
        body(Slot(at))
    with eng.Fori(0, 6) as i:
        body(Slot(1, i))
        body(Slot(2, i + 1))
    for at in (13, 14, 15, 16):
        body(Slot(at))
    with eng.Fori(0, 6) as i:
        body(Slot(17, i + 8))
        body(Slot(18, i + 9))
    for at in (29, 30, 31, 32):
        body(Slot(at))


def work_bank(s, i):
    return (i + len(WORK) * s.odd) % 2


def ended(s, h):
    for i, (kind, k, ahead, steps) in enumerate(WORK):
        if max(steps) == h and s.step(ahead).real:
            yield work_bank(s, i), kind, k, s.step(ahead)


def w_split(layer, name):
    return 2 * (4 * layer + WN.index(name) + 1)


def row3(ap, b):
    return ap[bass.ds(b, 1), :, :].rearrange("o p d -> (o p) d")


def attention_layers(nc, a, hidden, ident, ident_ready):
    with ExitStack() as ctx:
        def sb(name, shape, dt=F32):
            return ctx.enter_context(nc.sbuf_tensor(name, shape, dt))

        def ps(name, shape):
            return ctx.enter_context(nc.psum_tensor(name, shape, F32))

        def sem(name):
            return ctx.enter_context(nc.semaphore(name))

        w_hi = {x: sb(f"w{x}_hi", [128, C, D], F32R) for x in WN}
        w_lo = {x: sb(f"w{x}_lo", [128, C, D], F32R) for x in WN}
        w_stage = sb("w_stage", [128, 2, C // 2, D])
        ctx_g, ctx_b = sb("ctx_g", [128, C]), sb("ctx_b", [128, C])
        ln1_g, ln1_b = sb("ln1_g", [T, D]), sb("ln1_b", [T, D])
        q_bias, o_bias = sb("q_bias", [T, D]), sb("o_bias", [T, D])
        k_bias, v_bias = sb("k_bias", [128, C]), sb("v_bias", [128, C])
        gate = sb("gate", [128, 1])
        ctx_in = sb("ctx_in", [KR, KT, D])
        x_in = sb("x_in", [T, D])
        ctx_st, ctx_mv = sb("ctx_st", [KR, KT, 6]), sb("ctx_mv", [KR, KT, 2])
        ctx_rs, ctx_nm = sb("ctx_rs", [KR, KT]), sb("ctx_nm", [KR, KT])
        x_st, x_mv, x_rs = sb("x_st", [T, 6]), sb("x_mv", [T, 2]), sb("x_rs", [T, 1])
        ctx_ve, x_ve = sb("ctx_ve", [KR, KT]), sb("x_ve", [T, 1])
        eps, minus_half = sb("eps", [128, 1]), sb("minus_half", [128, 1])
        cT_hi, cT_lo = sb("cT_hi", [128, C, SP + 1], F32R), sb("cT_lo", [128, C, SP + 1], F32R)
        c32 = sb("c32", [128, 2, SP])
        xT_hi, xT_lo = sb("xT_hi", [128, C, T], F32R), sb("xT_lo", [128, C, T], F32R)
        q32 = sb("q32", [T, D])
        qT_hi, qT_lo = sb("qT_hi", [128, G, T], F32R), sb("qT_lo", [128, G, T], F32R)
        kT_hi, kT_lo = sb("kT_hi", [128, 2, SE], F32R), sb("kT_lo", [128, 2, SE], F32R)
        q_st = sb("q_st", [96, 2, GH, G, T], F32R)
        k_st = sb("k_st", [96, H, SE], F32R)
        v32 = sb("v32", [KR, 2, KT, D])
        mask8 = sb("mask8", [T, S], U8)
        minus_one, big = sb("minus_one", [T, 1]), sb("big", [T, 1])
        mask_add = sb("mask_add", [T, 2, S])
        p = sb("p", [T, 4, SP])
        p_min, p_sum, p_rec = sb("p_min", [T, 4]), sb("p_sum", [T, 4]), sb("p_rec", [T, 4])
        pT = sb("pT", [KR, 2, KT, GH, T])
        ao32 = sb("ao32", [128, G, T])
        ao_hi, ao_lo = sb("ao_hi", [128, G, T], F32R), sb("ao_lo", [128, G, T], F32R)
        res = sb("res", [T, D])
        x_out = sb("x_out", [T, D])

        work = ps("work", [128, 2, 512])
        side = ps("side", [128, 512])
        scores = ps("scores", [128, 2, 512])
        turned = ps("turned", [128, 2, 512])
        mixed = ps("mixed", [128, 512])

        consts1_in = sem("consts1_in")
        consts_in, w_in = sem("consts_in"), [sem("w_in0"), sem("w_in1")]
        ctx_loaded, x_loaded, mask_loaded, res_loaded = (
            sem("ctx_loaded"), sem("x_loaded"), sem("mask_loaded"), sem("res_loaded"))
        q_stacked = sem("q_stacked")
        k_stacked = [sem(f"k_stacked{g}") for g in range(G)]
        x_stored = sem("x_stored")
        gate_done, w_hi_done = sem("gate_done"), sem("w_hi_done")
        ctx_scaled = sem("ctx_scaled")
        cT_hi_done, xT_hi_done, qT_hi_done, kT_hi_done = (
            sem("cT_hi_done"), sem("xT_hi_done"), sem("qT_hi_done"), sem("kT_hi_done"))
        v_done, exp_done, pT_done, ao_hi_done = (
            sem("v_done"), sem("exp_done"), sem("pT_done"), sem("ao_hi_done"))
        w_lo_done = sem("w_lo_done")
        ctx_stats, ctx_aggr, ctx_rstd, ctx_shift = (
            sem("ctx_stats"), sem("ctx_aggr"), sem("ctx_rstd"), sem("ctx_shift"))
        x_stats, x_aggr, x_rstd, x_scaled = (
            sem("x_stats"), sem("x_aggr"), sem("x_rstd"), sem("x_scaled"))
        c32_done = sem("c32_done")
        cT_done, xT_done, q_done, qT_done, kT_done = (
            sem("cT_done"), sem("xT_done"), sem("q_done"), sem("qT_done"), sem("kT_done"))
        masked, rec_done, p_done = sem("masked"), sem("rec_done"), sem("p_done")
        ao32_done, ao_done, o_done = sem("ao32_done"), sem("ao_done"), sem("o_done")
        pads_done, mask_less_one, mask_lowest, mask_ready = (
            sem("pads_done"), sem("mask_less_one"), sem("mask_lowest"), sem("mask_ready"))
        ctx_var, x_var = sem("ctx_var"), sem("x_var")
        x_weighted, x_ready, res_ready = sem("x_weighted"), sem("x_ready"), sem("res_ready")
        cT_made, xT_made, q_made, qT_made, k_made, v_made, o_made = (
            sem("cT_made"), sem("xT_made"), sem("q_made"), sem("qT_made"), sem("k_made"),
            sem("v_made"), sem("o_made"))
        s_made, pT_made, pv_made = sem("s_made"), sem("pT_made"), sem("pv_made")

        block = ctx.enter_context(nc.Block())

        @block.sync
        def _(sp):
            def constants():
                for dst, src in ((ctx_g, a["g0"]), (ctx_b, a["b0"]), (k_bias, a["k_b"]), (v_bias, a["v_b"])):
                    sp.dma_start(dst[:, :], src).then_inc(consts_in, 16)
                sp.dma_start(gate[:, :], a["gate"].rearrange("(o d) -> o d", o=1).broadcast_to([128, 1])).then_inc(consts_in, 16)

            def constants1():
                for dst, src in ((ln1_g, a["ln1_w"]), (ln1_b, a["ln1_b"]), (q_bias, a["q_b"]), (o_bias, a["cproj_b"])):
                    sp.dma_start(dst[:, :], src.rearrange("(o d) -> o d", o=1).broadcast_to([T, D])).then_inc(consts1_in, 16)

            def weights(layer, name):
                src = a[f"w{layer}{name}"].rearrange("(j c p) n -> j p c n", j=2, p=128)
                for j in range(2):
                    at_least(sp, w_lo_done, w_split(layer, name) - 3 + j)
                    sp.dma_start(w_stage[:, j, :, :], src[j, :, :, :]).then_inc(w_in[j], 16)

            def stack_k(y, g):
                at_least(sp, kT_done, G * y.n + g + 1)
                for part, src in enumerate((kT_hi, kT_hi, kT_lo)):
                    dst = k_st[HD * part:HD * (part + 1), GH * g:GH * (g + 1), :]
                    sp.dma_start(dst.bitcast(F32), src[:, g % 2, :].bitcast(F32)).then_inc(k_stacked[g], 16)

            def body(s):
                n, m, z = s.step(1), s.step(2), s.step(-1)
                if s.at == 14:
                    weights(1, "q")
                if m.real:
                    at_least(sp, xT_made, n.n + 1)
                    if m.layer == 1:
                        at_least(sp, x_stored, 16 * (m.b + 1))
                    sp.dma_start(x_in[:, :], row3(a["x"] if m.layer == 0 else hidden, m.b)).then_inc(x_loaded, 16)
                if s.at == -1:
                    weights(0, "v")
                if s.real:
                    stack_k(s, G - 1)
                if s.at == 15:
                    weights(1, "v")
                if n.real:
                    at_least(sp, mask_ready, n.n)
                if m.real:
                    at_least(sp, cT_made, C * n.n + C)
                    sp.dma_start(ctx_in[:, :, :], a["ctx"][bass.ds(m.b, 1), :, :, :].rearrange("o k p d -> p (o k) d")).then_inc(ctx_loaded, 16)
                if n.real:
                    sp.dma_start(mask8[:, :], a["mask"][bass.ds(n.b, 1), :].broadcast_to([T, S])).then_inc(mask_loaded, 16)
                if s.at == -2:
                    weights(0, "q")
                    constants()
                    weights(0, "k")
                if s.at == -1:
                    weights(0, "o")
                    constants1()
                if s.at == 14:
                    weights(1, "k")
                if s.at == 15:
                    weights(1, "o")
                if z.real:
                    at_least(sp, o_done, z.n + 1)
                    sp.dma_start(row3(hidden, z.b), x_out[:, :]).then_inc(x_stored, 16)
                if s.real:
                    sp.dma_start(res[:, :], row3(a["x"] if s.layer == 0 else hidden, s.b)).then_inc(res_loaded, 16)
                if n.real:
                    at_least(sp, qT_done, n.n + 1)
                    for part, src in enumerate((qT_hi, qT_lo, qT_hi)):
                        sp.dma_start(q_st[HD * part:HD * (part + 1), n.odd, :, :, :].bitcast(F32), src[:, :, :].bitcast(F32)).then_inc(q_stacked, 16)
                    for g in range(G - 1):
                        stack_k(n, g)

            slots(sp, body)
            sp.wait_ge(x_stored, 16 * NS)

        @block.gpsimd
        def _(pool):
            pool.memset(p[:, :, S:SP], 0.0).then_inc(pads_done, 1)
            pool.memset(minus_one[:, :], -1.0).then_inc(pads_done, 1)
            pool.memset(big[:, :], BIG).then_inc(pads_done, 1)
            pool.memset(eps[:, :], EPS).then_inc(pads_done, 1)
            pool.memset(minus_half[:, :], -0.5).then_inc(pads_done, 1)
            pool.wait_ge(pads_done, 5)

            def body(s):
                n, m, z = s.step(1), s.step(2), s.step(-1)
                if s.at == 13:
                    pool.wait_ge(consts1_in, 16 * 4)
                if n.real and n.layer == 0:
                    for c in range(C):
                        pool.wait_ge(c32_done, C * n.n + c + 1)
                        pool.tensor_tensor(cT_lo[:, c, 0:SP], c32[:, c % 2, :], cT_hi[:, c, 0:SP].bitcast(F32), ALU.subtract).then_inc(cT_done, 1)
                if n.real:
                    pool.wait_ge(mask_loaded, 16 * (n.n + 1))
                    at_least(pool, masked, H * s.n)
                    half = mask_add[:, n.odd, :]
                    pool.tensor_tensor(half, mask8[:, :], minus_one[:, :].broadcast_to([T, S]), ALU.add).then_inc(mask_less_one, 1)
                    pool.wait_ge(mask_less_one, n.n + 1)
                    lowest = pool.tensor_tensor(half, half, big[:, :].broadcast_to([T, S]), ALU.mult)
                    lowest.then_inc(mask_lowest if n.layer == 0 else mask_ready, 1)
                    if n.layer == 0:
                        pool.wait_ge(mask_lowest, n.n + 1)
                        pool.tensor_tensor(half, half, half, ALU.add).then_inc(mask_ready, 1)
                if m.real and m.layer == 0:
                    pool.wait_ge(ctx_aggr, KT * (m.n + 1))
                    pool.tensor_tensor(ctx_ve[:, :], ctx_mv[:, :, 1], eps[0:KR, :].broadcast_to([KR, KT]), ALU.add).then_inc(ctx_var, 1)
                    pool.wait_ge(ctx_var, m.n + 1)
                    pool.tensor_tensor(ctx_rs[:, :], ctx_ve[:, :], minus_half[0:KR, :].broadcast_to([KR, KT]), ALU.pow).then_inc(ctx_rstd, 1)
                if m.real and m.layer == 1:
                    pool.wait_ge(x_aggr, m.b + 1)
                    pool.tensor_tensor(x_ve[:, :], x_mv[:, 1:2], eps[0:T, :], ALU.add).then_inc(x_var, 1)
                    pool.wait_ge(x_var, m.b + 1)
                    pool.tensor_tensor(x_rs[:, :], x_ve[:, :], minus_half[0:T, :], ALU.pow).then_inc(x_rstd, 1)
                    pool.wait_ge(x_scaled, m.b + 1)
                    pool.tensor_tensor(x_in[:, :], x_in[:, :], ln1_g[:, :], ALU.mult).then_inc(x_weighted, 1)
                    pool.wait_ge(x_weighted, m.b + 1)
                    pool.tensor_tensor(x_in[:, :], x_in[:, :], ln1_b[:, :], ALU.add).then_inc(x_ready, 1)
                if s.real and s.layer == 1:
                    pool.wait_ge(res_loaded, 16 * (s.n + 1))
                    pool.tensor_tensor(res[:, :], res[:, :], o_bias[:, :], ALU.add).then_inc(res_ready, 1)

            slots(pool, body)

        @block.scalar
        def _(act):
            def split_weights(layer, name):
                at = w_split(layer, name) - 2
                if layer:
                    act.wait_ge({"q": q_made, "k": k_made, "v": v_made, "o": o_made}[name], B * {"q": 1, "k": G, "v": KT, "o": 1}[name])
                for j in range(2):
                    act.wait_ge(w_in[j], 16 * (at // 2 + 1))
                    act.copy(w_hi[name][:, j * C // 2:(j + 1) * C // 2, :], w_stage[:, j, :, :]).then_inc(w_hi_done, 1)

            def context_affine(y, k):
                act.wait_ge(ctx_shift, y.n + 1)
                act.activation(ctx_in[:, k, :], ctx_in[:, k, :], ACT.Identity, bias=ctx_nm[:, k:k + 1], scale=ctx_rs[:, k:k + 1]).then_inc(ctx_scaled, 1)

            def body(s):
                n, m, z = s.step(1), s.step(2), s.step(-1)
                for h in range(H):
                    if s.real:
                        act.wait_ge(masked, H * s.n + h + 1)
                        act.activation(p[:, h % 4, 0:S], p[:, h % 4, 0:S], ACT.Exp, bias=p_min[:, h % 4:h % 4 + 1], scale=-1.0,
                                       accum_out=p_sum[:, h % 4:h % 4 + 1]).then_inc(exp_done, 1)
                    if z.real and h == AO_AT + 1:
                        act.wait_ge(ao32_done, z.n + 1)
                        at_least(act, o_made, z.n)
                        act.copy(ao_hi[:, :, :], ao32[:, :, :]).then_inc(ao_hi_done, 1)
                    for bank, kind, k, y in ended(s, h):
                        if kind == "K":
                            act.wait_ge(k_made, G * y.n + k + 1)
                            at_least(act, k_stacked[(k + 2) % G], 16 * PARTS * (y.n + k // 2))
                            src = work[:, bank, 0:SE]
                            if y.layer == 0:
                                act.copy(kT_hi[:, k % 2, :], src).then_inc(kT_hi_done, 1)
                            else:
                                act.activation(kT_hi[:, k % 2, :], src, ACT.Identity, bias=k_bias[:, k:k + 1]).then_inc(kT_hi_done, 1)
                        if kind == "V":
                            act.wait_ge(v_made, KT * y.n + k + 1)
                            at_least(act, pv_made, G * (y.n - 1))
                            act.copy(v32[:, y.odd, k, :], work[0:KR, bank, :]).then_inc(v_done, 1)
                    if n.real and h == XT_AT:
                        act.wait_ge(xT_made, n.n + 1)
                        at_least(act, q_made, n.n)
                        act.copy(xT_hi[:, :, :], side[:, 0:C * T].rearrange("p (c t) -> p c t", c=C)).then_inc(xT_hi_done, 1)
                    if n.real and n.layer == 0 and h < KT - 1:
                        context_affine(n, h + 1)
                    if s.at == -1 and h == XT_AT:
                        act.wait_ge(consts_in, 16 * 5)
                        act.activation(gate[:, :], gate[:, :], ACT.Tanh).then_inc(gate_done, 1)
                    if n.real and h in T_AT:
                        c = T_AT[h]
                        act.wait_ge(cT_made, C * n.n + c + 1)
                        at_least(act, k_made, G * n.n)
                        at_least(act, v_made, KT * n.n)
                        if n.layer == 0:
                            act.activation(cT_hi[:, c, 0:SP], side[:, 0:SP], ACT.Identity, bias=ctx_b[:, c:c + 1], scale=ctx_g[:, c:c + 1]).then_inc(cT_hi_done, 1)
                        else:
                            act.copy(cT_hi[:, c, 0:SP], side[:, 0:SP]).then_inc(cT_hi_done, 1)
                    if n.real and h == QT_AT:
                        act.wait_ge(qT_made, n.n + 1)
                        at_least(act, q_stacked, 16 * PARTS * n.n)
                        act.copy(qT_hi[:, :, :], side[:, 0:G * T].rearrange("p (c t) -> p c t", c=G)).then_inc(qT_hi_done, 1)
                    y, hh = (s, h - LAG) if h >= LAG else (z, h - LAG + H)
                    if y.real:
                        act.wait_ge(pT_made, H * y.n + hh + 1)
                        g, j = hh // GH, hh % GH
                        if j == 0:
                            at_least(act, pv_made, G * y.n + g - 1)
                        act.copy(pT[:, g % 2, :, j, :], turned[0:KR, hh % 2, 0:KT * T].rearrange("p (k t) -> p k t", k=KT)).then_inc(pT_done, 1)
                    if m.real and m.layer == 0 and h == H - 1:
                        context_affine(m, 0)
                    if (s.at, h) in SPLIT_AT:
                        split_weights(*SPLIT_AT[s.at, h])
                    if s.at == NS and h == O_END:
                        break

            slots(act, body)

        @block.vector
        def _(dve):
            dve.wait_ge(pads_done, 5)

            def split_weights(layer, name):
                at = w_split(layer, name) - 2
                for j in range(2):
                    dve.wait_ge(w_hi_done, at + j + 1)
                    c = slice(j * C // 2, (j + 1) * C // 2)
                    dve.tensor_tensor(w_lo[name][:, c, :], w_stage[:, j, :, :], w_hi[name][:, c, :].bitcast(F32), ALU.subtract).then_inc(w_lo_done, 1)

            def body(s):
                n, m, z = s.step(1), s.step(2), s.step(-1)
                if s.at == -1:
                    dve.wait_ge(gate_done, 1)
                for h in range(H):
                    y, hh = (s, h - 1) if h else (z, H - 1)
                    if s.real:
                        if h == 0:
                            dve.wait_ge(mask_ready, s.n + 1)
                        dve.wait_ge(s_made, H * s.n + h + 1)
                        at_least(dve, pT_made, H * s.n + h - 3)
                    if m.real and m.layer == 0 and h == CTX_AGGR_AT:
                        dve.wait_ge(ctx_stats, KT * (m.n + 1))
                    if m.real and m.layer == 1 and h == X_AGGR_AT:
                        dve.wait_ge(x_stats, m.b + 1)
                    if y.real:
                        dve.wait_ge(exp_done, H * y.n + hh + 1)
                        dve.reciprocal(p_rec[:, hh % 4:hh % 4 + 1], p_sum[:, hh % 4:hh % 4 + 1]).then_inc(rec_done, 1)
                    if s.real:
                        dve.tensor_tensor_reduce(out=p[:, h % 4, 0:S], in0=scores[0:T, h % 2, 0:S], in1=mask_add[:, s.odd, :],
                                                 scale=-SCALE, scalar=BIG, op0=ALU.add, op1=ALU.min,
                                                 accum_out=p_min[:, h % 4:h % 4 + 1]).then_inc(masked, 1)
                    if y.real:
                        dve.wait_ge(rec_done, H * y.n + hh + 1)
                        dve.tensor_scalar(p[:, hh % 4, 0:S], p[:, hh % 4, 0:S], p_rec[:, hh % 4:hh % 4 + 1], None, ALU.mult).then_inc(p_done, 1)
                    for bank, kind, k, v in ended(s, h):
                        if kind == "K":
                            dve.wait_ge(kT_hi_done, G * v.n + k + 1)
                            src = work[:, bank, 0:SE]
                            hi = kT_hi[:, k % 2, :].bitcast(F32)
                            if v.layer == 0:
                                dve.tensor_tensor(kT_lo[:, k % 2, :], src, hi, ALU.subtract).then_inc(kT_done, 1)
                            else:
                                dve.scalar_tensor_tensor(kT_lo[:, k % 2, :], src, k_bias[:, k:k + 1], hi, ALU.add, ALU.subtract).then_inc(kT_done, 1)
                        if kind == "Q":
                            dve.wait_ge(q_made, v.n + 1)
                            at_least(dve, qT_made, v.n)
                            if v.layer == 0:
                                dve.tensor_copy(q32[:, :], work[0:T, bank, :]).then_inc(q_done, 1)
                            else:
                                dve.tensor_tensor(q32[:, :], work[0:T, bank, :], q_bias[:, :], ALU.add).then_inc(q_done, 1)
                        if kind == "O":
                            dve.wait_ge(o_made, v.n + 1)
                            at_least(dve, x_stored, 16 * v.n)
                            if v.layer == 0:
                                dve.wait_ge(res_loaded, 16 * (v.n + 1))
                                dve.scalar_tensor_tensor(x_out[:, :], work[0:T, bank, :], gate[0:T, :], res[:, :], ALU.mult, ALU.add).then_inc(o_done, 1)
                            else:
                                dve.wait_ge(res_ready, v.b + 1)
                                dve.tensor_tensor(x_out[:, :], work[0:T, bank, :], res[:, :], ALU.add).then_inc(o_done, 1)
                    if n.real and h == XT_AT:
                        dve.wait_ge(xT_hi_done, n.n + 1)
                        dve.tensor_tensor(xT_lo[:, :, :], side[:, 0:C * T].rearrange("p (c t) -> p c t", c=C), xT_hi[:, :, :].bitcast(F32), ALU.subtract).then_inc(xT_done, 1)
                    if n.real and h in T_AT:
                        c = T_AT[h]
                        dve.wait_ge(cT_hi_done, C * n.n + c + 1)
                        if n.layer == 0:
                            if c >= 2:
                                dve.wait_ge(cT_done, C * n.n + c - 1)
                            dve.tensor_scalar(c32[:, c % 2, :], side[:, 0:SP], ctx_g[:, c:c + 1], ctx_b[:, c:c + 1], ALU.mult, ALU.add).then_inc(c32_done, 1)
                        else:
                            dve.tensor_tensor(cT_lo[:, c, 0:SP], side[:, 0:SP], cT_hi[:, c, 0:SP].bitcast(F32), ALU.subtract).then_inc(cT_done, 1)
                    if n.real and h == QT_AT:
                        dve.wait_ge(qT_hi_done, n.n + 1)
                        dve.tensor_tensor(qT_lo[:, :, :], side[:, 0:G * T].rearrange("p (c t) -> p c t", c=G), qT_hi[:, :, :].bitcast(F32), ALU.subtract).then_inc(qT_done, 1)
                    if z.real and h == AO_AT:
                        dve.wait_ge(pv_made, G * z.n + G)
                        src = mixed[:, 0:G * T].rearrange("p (g t) -> p g t", g=G)
                        if z.layer == 0:
                            dve.tensor_copy(ao32[:, :, :], src).then_inc(ao32_done, 1)
                        else:
                            dve.tensor_tensor(ao32[:, :, :], src, v_bias[:, :].unsqueeze(2).broadcast_to([128, G, T]), ALU.add).then_inc(ao32_done, 1)
                    if z.real and h == AO_AT + 1:
                        dve.wait_ge(ao_hi_done, z.n + 1)
                        dve.tensor_tensor(ao_lo[:, :, :], ao32[:, :, :], ao_hi[:, :, :].bitcast(F32), ALU.subtract).then_inc(ao_done, 1)
                    if m.real and m.layer == 0:
                        if h in CTX_STATS_AT:
                            k = CTX_STATS_AT[h]
                            dve.wait_ge(ctx_loaded, 16 * (m.n + 1))
                            dve.bn_stats(ctx_st[:, k, :], ctx_in[:, k, :]).then_inc(ctx_stats, 1)
                        if h == CTX_AGGR_AT:
                            for k in range(KT):
                                dve.bn_aggr(ctx_mv[:, k, :], ctx_st[:, k, :]).then_inc(ctx_aggr, 1)
                        if h == CTX_SHIFT_AT:
                            dve.wait_ge(ctx_rstd, m.n + 1)
                            dve.scalar_tensor_tensor(ctx_nm[:, :], ctx_mv[:, :, 0], -1.0, ctx_rs[:, :], ALU.mult, ALU.mult).then_inc(ctx_shift, 1)
                    if m.real and m.layer == 1:
                        if h == X_STATS_AT:
                            dve.wait_ge(x_loaded, 16 * (m.n + 1))
                            dve.bn_stats(x_st[:, :], x_in[:, :]).then_inc(x_stats, 1)
                        if h == X_AGGR_AT:
                            dve.bn_aggr(x_mv[:, :], x_st[:, :]).then_inc(x_aggr, 1)
                        if h == X_SCALE_AT:
                            dve.wait_ge(x_rstd, m.b + 1)
                            dve.tensor_scalar(x_in[:, :], x_in[:, :], x_mv[:, 0:1], x_rs[:, 0:1], ALU.subtract, ALU.mult).then_inc(x_scaled, 1)
                    if (s.at, h) in SPLIT_AT:
                        split_weights(*SPLIT_AT[s.at, h])

            slots(dve, body)

        @block.tensor
        def _(pe):
            pe.wait_ge(ident_ready, 2)

            def pieces(out, pairs, first, last):
                todo = [(x, y) for (x_hi, x_lo, y_hi, y_lo) in pairs for (x, y) in ((x_hi, y_hi), (x_hi, y_lo), (x_lo, y_hi))]
                for i in range(first, last):
                    made = pe.matmul(out, *todo[i], start=i == 0, stop=i == len(todo) - 1)
                return made

            def bank_free(s, i):
                while s.at >= -1:
                    i -= 2
                    if i < 0:
                        s, i = s.step(-1), i + len(WORK)
                    kind, k, ahead, _ = WORK[i]
                    y = s.step(ahead)
                    if y.real:
                        done, per = {"K": (kT_done, G), "V": (v_done, KT), "Q": (q_done, 1), "O": (o_done, 1)}[kind]
                        pe.wait_ge(done, per * y.n + k + 1)
                        return

            def work_item(s, i, h):
                kind, k, ahead, steps = WORK[i]
                y = s.step(ahead)
                if not y.real or h not in steps:
                    return
                if h == min(steps):
                    bank_free(s, i)
                    if kind == "Q":
                        pe.wait_ge(xT_done, y.n + 1)
                    elif kind == "O":
                        pe.wait_ge(ao_done, y.n + 1)
                    else:
                        pe.wait_ge(cT_done, C * y.n + C)
                    pe.wait_ge(w_lo_done, w_split(y.layer, kind.lower()))
                bank = work[:, work_bank(s, i), :]
                if kind == "Q":
                    out, made = bank[0:T, :], q_made
                    pairs = [(xT_hi[:, c, :], xT_lo[:, c, :], w_hi["q"][:, c, :], w_lo["q"][:, c, :]) for c in range(C)]
                elif kind == "K":
                    out, made, w = bank[:, 0:SE], k_made, slice(k * 128, (k + 1) * 128)
                    pairs = [(w_hi["k"][:, c, w], w_lo["k"][:, c, w], cT_hi[:, c, 0:SE], cT_lo[:, c, 0:SE]) for c in range(C)]
                elif kind == "V":
                    out, made, r = bank[0:KR, :], v_made, slice(k * KR, (k + 1) * KR)
                    pairs = [(cT_hi[:, c, r], cT_lo[:, c, r], w_hi["v"][:, c, :], w_lo["v"][:, c, :]) for c in range(C)]
                else:
                    out, made = bank[0:T, :], o_made
                    pairs = [(ao_hi[:, c, :], ao_lo[:, c, :], w_hi["o"][:, c, :], w_lo["o"][:, c, :]) for c in range(C)]
                first = sum(count for step, count in steps.items() if step < h)
                last = pieces(out, pairs, first, first + steps[h])
                if h == max(steps):
                    last.then_inc(made, 1)

            def body(s):
                n, z = s.step(1), s.step(-1)
                for h in range(H):
                    if s.real:
                        if h == 0:
                            pe.wait_ge(q_stacked, 16 * PARTS * (s.n + 1))
                        if h % GH == 0:
                            pe.wait_ge(k_stacked[h // GH], 16 * PARTS * (s.n + 1))
                        at_least(pe, masked, H * s.n + h - 1)
                        pe.matmul(scores[0:T, h % 2, 0:SE], q_st[:, s.odd, h % GH, h // GH, :], k_st[:, h, :], start=True, stop=True).then_inc(s_made, 1)
                    for i in range(len(WORK)):
                        work_item(s, i, h)
                    if h in PV_AT:
                        g = PV_AT[h]
                        y = z if g == G - 1 else s
                        if y.real:
                            pe.wait_ge(pT_done, H * y.n + GH * (g + 1))
                            if g == 0:
                                pe.wait_ge(v_done, KT * (y.n + 1))
                                at_least(pe, ao32_done, y.n)
                            for k in range(KT):
                                for j in range(GH):
                                    hd = (GH * g + j) * HD
                                    last = pe.matmul(mixed[32 * j:32 * j + 32, g * T:(g + 1) * T], v32[:, y.odd, k, hd:hd + HD], pT[:, g % 2, k, j, :],
                                                     start=k == 0, stop=k == KT - 1)
                            last.then_inc(pv_made, 1)
                    if n.real and h == XT_AT:
                        if n.layer == 0:
                            pe.wait_ge(x_loaded, 16 * (n.n + 1))
                        else:
                            pe.wait_ge(x_ready, n.b + 1)
                        at_least(pe, qT_done, n.n)
                        for c in range(C):
                            last = pe.transpose(side[:, c * T:(c + 1) * T], x_in[:, c * 128:(c + 1) * 128], ident[0:T, 0:T])
                        last.then_inc(xT_made, 1)
                    if n.real and h in T_AT:
                        c = T_AT[h]
                        if c == 0:
                            if n.layer == 0:
                                pe.wait_ge(ctx_scaled, KT * (n.n + 1))
                            else:
                                pe.wait_ge(ctx_loaded, 16 * (n.n + 1))
                            pe.wait_ge(xT_done, n.n + 1)
                        else:
                            pe.wait_ge(c32_done if n.layer == 0 else cT_done, C * n.n + c)
                        for k in range(KT):
                            last = pe.transpose(side[:, k * KR:(k + 1) * KR], ctx_in[:, k, c * 128:(c + 1) * 128], ident[0:KR, 0:KR])
                        last.then_inc(cT_made, 1)
                    if n.real and h == QT_AT:
                        pe.wait_ge(q_done, n.n + 1)
                        pe.wait_ge(c32_done if n.layer == 0 else cT_done, C * n.n + C)
                        for g in range(G):
                            last = pe.transpose(side[:, g * T:(g + 1) * T], q32[:, g * 128:(g + 1) * 128], ident[0:T, 0:T])
                        last.then_inc(qT_made, 1)
                    y, hh = (s, h - LAG) if h >= LAG else (z, h - LAG + H)
                    if y.real:
                        pe.wait_ge(p_done, H * y.n + hh + 1)
                        at_least(pe, pT_done, H * y.n + hh - 1)
                        for k in range(KT):
                            last = pe.transpose(turned[0:KR, hh % 2, k * T:(k + 1) * T], p[:, hh % 4, k * KR:(k + 1) * KR], ident[0:T, 0:T])
                        last.then_inc(pT_made, 1)
                    if s.at == NS and h == O_END:
                        break

            slots(pe, body)


def mlp(nc, a, hidden, out, ident):
    with ExitStack() as ctx:
        def sb(name, shape, dt=F32):
            return ctx.enter_context(nc.sbuf_tensor(name, shape, dt))

        def sem(name):
            return ctx.enter_context(nc.semaphore(name))

        WP = 2 * C
        N = MG * T
        wf_hi, wf_lo = sb("wf_hi", [128, C, F], F32R), sb("wf_lo", [128, C, F], F32R)
        wp_hi, wp_lo = sb("wp_hi", [128, FC, D], F32R), sb("wp_lo", [128, FC, D], F32R)
        stage = sb("stage", [128, 2, F])
        ln2_g, ln2_b, p_bias = sb("ln2_g", [T, D]), sb("ln2_b", [T, D]), sb("p_bias", [T, D])
        f_bias = sb("f_bias", [128, FC])
        x2, y = sb("x2", [T, MG, D]), sb("y", [T, MG, D])
        st, mv, rs = sb("st", [T, MG, 6]), sb("mv", [T, MG, 2]), sb("rs", [T, MG])
        after_stats = sb("after_stats", [T, 1])
        ve, eps, minus_half = sb("ve", [T, MG]), sb("mlp_eps", [T, 1]), sb("mlp_minus_half", [T, 1])
        yT_hi, yT_lo = sb("yT_hi", [128, C, N], F32R), sb("yT_lo", [128, C, N], F32R)
        h32 = sb("h32", [128, 2, N])
        h_hi, h_lo = sb("h_hi", [128, 2, N], F32R), sb("h_lo", [128, 2, N], F32R)
        turned = ctx.enter_context(nc.psum_tensor("mlp_turned", [128, 2, 512], F32))
        up = ctx.enter_context(nc.psum_tensor("mlp_up", [128, 2, 512], F32))
        down = ctx.enter_context(nc.psum_tensor("mlp_down", [128, MG, 512], F32))

        consts_in, w_in0, w_in1, x_in, stored = (
            sem("mlp_consts_in"), sem("mlp_w_in0"), sem("mlp_w_in1"), sem("mlp_x_in"), sem("stored"))
        w_in = (w_in0, w_in1)
        w_hi_done, w_lo_done = sem("mlp_w_hi_done"), sem("mlp_w_lo_done")
        stats_done, aggr_done, rstd_done, scaled, weighted, y_ready, res_ready = (
            sem("mlp_stats"), sem("mlp_aggr"), sem("mlp_rstd"), sem("mlp_scaled"), sem("mlp_weighted"),
            sem("mlp_y_ready"), sem("mlp_res_ready"))
        pads_done, var_done = sem("mlp_pads_done"), sem("mlp_var_done")
        yT_made, yT_hi_done, yT_done = sem("yT_made"), sem("yT_hi_done"), sem("yT_done")
        up_made, gelu_done, h_hi_done, h_done, down_made, out_done = (
            sem("up_made"), sem("gelu_done"), sem("h_hi_done"), sem("h_done"), sem("down_made"), sem("out_done"))

        block = ctx.enter_context(nc.Block())

        def groups(eng, body):
            body(-1)
            body(0, True)
            with eng.Fori(1, NG - 1) as i:
                body(i, True)
            body(NG - 1)

        @block.sync
        def _(sp):
            hid = hidden.rearrange("(g m) t d -> g t m d", m=MG)
            dst = out.rearrange("(g m) t d -> g t m d", m=MG)

            def load(g):
                at_least(sp, stored, 16 * g)
                sp.dma_start(x2[:, :, :], hid[bass.ds(g, 1), :, :, :].rearrange("o t m d -> t (o m) d")).then_inc(x_in, 16)

            for dstv, src in ((ln2_g, a["ln2_w"]), (ln2_b, a["ln2_b"]), (p_bias, a["proj_b"])):
                sp.dma_start(dstv[:, :], src.rearrange("(o d) -> o d", o=1).broadcast_to([T, D])).then_inc(consts_in, 16)
            sp.dma_start(f_bias[:, :], a["fc_b"]).then_inc(consts_in, 16)
            load(0)
            fc = a["fc_w"].rearrange("(c p) n -> c p n", p=128)
            pr = a["proj_w"].rearrange("(k c p) n -> k p c n", p=128, k=C)
            for k in range(WP):
                at_least(sp, w_lo_done, k - 1)
                src = fc[k, :, :] if k < C else pr[k - C, :, :, :]
                d = stage[:, k % 2, :] if k < C else stage[:, k % 2, :].rearrange("p (c n) -> p c n", n=D)
                sp.dma_start(d, src).then_inc(w_in[k % 2], 16)

            def body(g, more=False):
                if isinstance(g, int) and g < 0:
                    return
                sp.wait_ge(out_done, MG * (g + 1))
                sp.dma_start(dst[bass.ds(g, 1), :, :, :].rearrange("o t m d -> t (o m) d"), x2[:, :, :]).then_inc(stored, 16)
                if more:
                    load(g + 1)

            groups(sp, body)
            sp.wait_ge(stored, 16 * NG)

        @block.gpsimd
        def _(pool):
            pool.wait_ge(consts_in, 16 * 4)
            pool.memset(eps[:, :], EPS).then_inc(pads_done, 1)
            pool.memset(minus_half[:, :], -0.5).then_inc(pads_done, 1)
            pool.wait_ge(pads_done, 2)

            def prepare(g):
                pool.wait_ge(aggr_done, MG * (g + 1))
                pool.tensor_tensor(ve[:, :], mv[:, :, 1], eps[:, :].broadcast_to([T, MG]), ALU.add).then_inc(var_done, 1)
                pool.wait_ge(var_done, g + 1)
                pool.tensor_tensor(rs[:, :], ve[:, :], minus_half[:, :].broadcast_to([T, MG]), ALU.pow).then_inc(rstd_done, 1)
                for i in range(MG):
                    pool.wait_ge(scaled, MG * g + i + 1)
                    pool.tensor_tensor(y[:, i, :], y[:, i, :], ln2_g[:, :], ALU.mult).then_inc(weighted, 1)
                    pool.wait_ge(weighted, MG * g + i + 1)
                    pool.tensor_tensor(y[:, i, :], y[:, i, :], ln2_b[:, :], ALU.add).then_inc(y_ready, 1)
                for i in range(MG):
                    pool.tensor_tensor(x2[:, i, :], x2[:, i, :], p_bias[:, :], ALU.add).then_inc(res_ready, 1)

            def body(g, more=False):
                if more or (isinstance(g, int) and g < 0):
                    prepare(g + 1)

            groups(pool, body)

        @block.scalar
        def _(act):
            act.wait_ge(consts_in, 16 * 4)
            for k in range(WP):
                act.wait_ge(w_in[k % 2], 16 * (k // 2 + 1))
                d = wf_hi[:, k, :] if k < C else wp_hi[:, C * (k - C):C * (k - C + 1), :]
                s = stage[:, k % 2, :] if k < C else stage[:, k % 2, :].rearrange("p (c n) -> p c n", n=D)
                act.copy(d, s).then_inc(w_hi_done, 1)

            def body(g, more=False):
                if isinstance(g, int) and g < 0:
                    return
                for c in range(C):
                    act.wait_ge(yT_made, C * g + c + 1)
                    at_least(act, up_made, FC * g)
                    act.copy(yT_hi[:, c, :], turned[:, c % 2, 0:N]).then_inc(yT_hi_done, 1)
                for k in range(FC):
                    act.wait_ge(up_made, FC * g + k + 1)
                    at_least(act, h_done, FC * g + k - 1)
                    act.activation(h32[:, k % 2, :], up[:, k % 2, 0:N], ACT.Gelu_apprx_tanh, bias=f_bias[:, k:k + 1]).then_inc(gelu_done, 1)
                    act.wait_ge(gelu_done, FC * g + k + 1)
                    at_least(act, down_made, FC * g + k - 1)
                    act.copy(h_hi[:, k % 2, :], h32[:, k % 2, :]).then_inc(h_hi_done, 1)

            groups(act, body)

        @block.vector
        def _(dve):
            def normalise(g):
                dve.wait_ge(x_in, 16 * (g + 1))
                for i in range(MG):
                    dve.bn_stats(st[:, i, :], x2[:, i, :]).then_inc(stats_done, 1)
                dve.wait_ge(stats_done, MG * (g + 1))
                dve.memset(after_stats[:, :], 0.0)
                for i in range(MG):
                    dve.bn_aggr(mv[:, i, :], st[:, i, :]).then_inc(aggr_done, 1)
                dve.wait_ge(rstd_done, g + 1)
                at_least(dve, yT_made, C * g)
                for i in range(MG):
                    dve.tensor_scalar(y[:, i, :], x2[:, i, :], mv[:, i, 0:1], rs[:, i:i + 1], ALU.subtract, ALU.mult).then_inc(scaled, 1)

            def split_weights(ks):
                for k in ks:
                    dve.wait_ge(w_hi_done, k + 1)
                    if k < C:
                        dve.tensor_tensor(wf_lo[:, k, :], stage[:, k % 2, :], wf_hi[:, k, :].bitcast(F32), ALU.subtract).then_inc(w_lo_done, 1)
                    else:
                        c = slice(C * (k - C), C * (k - C + 1))
                        dve.tensor_tensor(wp_lo[:, c, :], stage[:, k % 2, :].rearrange("p (c n) -> p c n", n=D), wp_hi[:, c, :].bitcast(F32), ALU.subtract).then_inc(w_lo_done, 1)

            def body(g, more=False):
                if isinstance(g, int) and g < 0:
                    normalise(0)
                    split_weights(range(WP))
                    return
                for c in range(C):
                    dve.wait_ge(yT_hi_done, C * g + c + 1)
                    dve.tensor_tensor(yT_lo[:, c, :], turned[:, c % 2, 0:N], yT_hi[:, c, :].bitcast(F32), ALU.subtract).then_inc(yT_done, 1)
                for k in range(FC):
                    dve.wait_ge(h_hi_done, FC * g + k + 1)
                    dve.tensor_tensor(h_lo[:, k % 2, :], h32[:, k % 2, :], h_hi[:, k % 2, :].bitcast(F32), ALU.subtract).then_inc(h_done, 1)
                dve.wait_ge(down_made, FC * (g + 1))
                dve.wait_ge(res_ready, MG * (g + 1))
                for i in range(MG):
                    dve.tensor_tensor(x2[:, i, :], down[0:T, i, :], x2[:, i, :], ALU.add).then_inc(out_done, 1)
                if more:
                    normalise(g + 1)

            groups(dve, body)

        @block.tensor
        def _(pe):
            def body(g, more=False):
                if isinstance(g, int) and g < 0:
                    return
                for c in range(C):
                    if c == 0:
                        pe.wait_ge(y_ready, MG * (g + 1))
                    if c >= 2:
                        pe.wait_ge(yT_done, C * g + c - 1)
                    else:
                        at_least(pe, yT_done, C * g)
                    for i in range(MG):
                        last = pe.transpose(turned[:, c % 2, i * T:(i + 1) * T], y[:, i, c * 128:(c + 1) * 128], ident[0:T, 0:T])
                    last.then_inc(yT_made, 1)
                for k in range(FC + 1):
                    if k < FC:
                        if k == 0:
                            pe.wait_ge(yT_done, C * (g + 1))
                            pe.wait_ge(w_lo_done, C)
                        at_least(pe, gelu_done, FC * g + k - 1)
                        f = slice(k * 128, (k + 1) * 128)
                        todo = [xy for c in range(C) for xy in ((wf_hi[:, c, f], yT_hi[:, c, :]), (wf_hi[:, c, f], yT_lo[:, c, :]), (wf_lo[:, c, f], yT_hi[:, c, :]))]
                        for i, (w, v) in enumerate(todo):
                            last = pe.matmul(up[:, k % 2, 0:N], w, v, start=i == 0, stop=i == len(todo) - 1)
                        last.then_inc(up_made, 1)
                    if k >= 1:
                        j = k - 1
                        pe.wait_ge(h_done, FC * g + j + 1)
                        if j == 0:
                            at_least(pe, out_done, MG * g)
                        if j % C == 0:
                            pe.wait_ge(w_lo_done, C + j // C + 1)
                        for i in range(MG):
                            t = slice(i * T, (i + 1) * T)
                            for e, (v, w) in enumerate(((h_hi[:, j % 2, t], wp_hi[:, j, :]), (h_hi[:, j % 2, t], wp_lo[:, j, :]), (h_lo[:, j % 2, t], wp_hi[:, j, :]))):
                                last = pe.matmul(down[0:T, i, :], v, w, start=j == 0 and e == 0, stop=j == FC - 1 and e == 2)
                        last.then_inc(down_made, 1)

            groups(pe, body)


def build(nc, a, out):
    hidden = nc.dram_tensor("hidden", [B, T, D], F32, kind="Internal").ap()
    with ExitStack() as ctx:
        ident = ctx.enter_context(nc.sbuf_tensor("ident", [128, 128], F32))
        ident_ready = ctx.enter_context(nc.semaphore("ident_ready"))
        with nc.Block() as block:
            @block.gpsimd
            def _(pool):
                pool.memset(ident[:, :], 0.0).then_inc(ident_ready, 1)
                pool.wait_ge(ident_ready, 1)
                pool.affine_select(out=ident[:, :], in_=ident[:, :], compare_op=ALU.not_equal, fill=1.0, base=0,
                                   pattern=[[-1, 128]], channel_multiplier=1).then_inc(ident_ready, 1)
        attention_layers(nc, a, hidden, ident, ident_ready)
        mlp(nc, a, hidden, out, ident)


def kernel(x, ctx_2048, mask_BxS2_bf1, **w):
    import numpy as np
    import concourse.bacc as bacc
    from concourse.bass_utils import run_bass_kernel_spmd

    ctx = np.zeros((B, SP, D), np.float32)
    ctx[:, :S, :] = np.asarray(ctx_2048)
    l0, l1 = "L0_xattn_", "L1_xattn_"

    def columns(v):
        return np.asarray(v).reshape(-1, 128).T

    def by_dim(v):
        v = np.asarray(v)
        return v.reshape(-1, G, GH, HD).transpose(0, 1, 3, 2).reshape(v.shape)

    named = {
        "x": x, "ctx": ctx.reshape(B, KT, KR, D), "mask": np.asarray(mask_BxS2_bf1).view(np.uint8),
        "w0q": by_dim(np.asarray(w[l0 + "Wq"]).T), "w0k": by_dim(np.asarray(w[l0 + "Wk"]).T), "w0v": np.asarray(w[l0 + "Wv"]).T,
        "w0o": np.asarray(w[l0 + "Wo"]).T, "g0": columns(w[l0 + "ln_gamma"]), "b0": columns(w[l0 + "ln_beta"]), "gate": w[l0 + "gate"],
        "w1q": by_dim(w[l1 + "q_w"]), "w1k": by_dim(w[l1 + "k_w"]), "w1v": w[l1 + "v_w"], "w1o": w[l1 + "cproj_w"],
        "ln1_w": w[l1 + "ln1_w"], "ln1_b": w[l1 + "ln1_b"], "q_b": by_dim(w[l1 + "q_b"]), "k_b": columns(by_dim(w[l1 + "k_b"])), "v_b": columns(w[l1 + "v_b"]),
        "cproj_b": w[l1 + "cproj_b"], "ln2_w": w[l1 + "ln2_w"], "ln2_b": w[l1 + "ln2_b"], "fc_w": w[l1 + "fc_w"],
        "fc_b": columns(w[l1 + "fc_b"]), "proj_w": w[l1 + "proj_w"], "proj_b": w[l1 + "proj_b"],
    }
    nc = bacc.Bacc("TRN2", target_bir_lowering=False, num_devices=1)
    arrays, a = {}, {}
    for name, value in named.items():
        value = np.ascontiguousarray(value)
        arrays[f"in_{name}"] = value
        a[name] = nc.dram_tensor(f"in_{name}", value.shape, mybir.dt.from_np(value.dtype), kind="ExternalInput").ap()
    out = nc.dram_tensor("out", [B, T, D], F32, kind="ExternalOutput").ap()
    build(nc, a, out)
    r = run_bass_kernel_spmd(nc, [arrays], core_ids=[0])
    return r.results[0]["out"]
```

```python
from contextlib import ExitStack

import concourse.bass as bass
from concourse import mybir

ALU = mybir.AluOpType
ACT = mybir.ActivationFunctionType
F32 = mybir.dt.float32
F32R = mybir.dt.float32r
U8 = mybir.dt.uint8

B, T, D = 16, 100, 512
S = 361
H, HD = 16, 32
C = D // 128
GH = 128 // HD
G = H // GH
KT = 3
KR = (S + KT - 1) // KT
SP = KT * KR
SE = S + S % 2
F = 2048
FC = F // 128
EPS = 1e-5
SCALE = HD ** -0.5
BIG = 3.3895313892515355e38
NS = 2 * B
MG = 4
NG = B // MG

XT_AT, T_AT, QT_AT = 0, {3: 0, 5: 1, 6: 2, 7: 3}, 9
WORK = (("K", 3, 0, {0: 8, 1: 4}), ("V", 2, 0, {1: 4, 2: 4, 3: 4}), ("Q", 0, 1, {4: 6, 5: 6}), ("O", 0, -1, {6: 8, 7: 4}),
        ("V", 0, 1, {8: 6, 9: 6}), ("K", 0, 1, {9: 2, 10: 10}), ("V", 1, 1, {11: 4, 12: 8}),
        ("K", 1, 1, {13: 11, 14: 1}), ("K", 2, 1, {14: 10, 15: 2}))
assert all(sum(steps.values()) == 3 * C for _, _, _, steps in WORK)
FIRST_CONTEXT_USE = WORK.index(next(item for item in WORK if item[:3] == ("V", 0, 1)))
O_END = next(max(steps) for kind, _, _, steps in WORK if kind == "O")
PV_AT = {7: 0, 11: 1, 15: 2, 2: 3}
AO_AT = 2
LAG = 2
CTX_STATS_AT, CTX_AGGR_AT, CTX_SHIFT_AT = {10: 0, 11: 1, 12: 2}, 13, 14
CTX_SCALE_AT = {15: (0, 2), 0: (1, 1), 1: (2, 1)}
X_STATS_AT, X_AGGR_AT, X_SCALE_AT = 8, 9, 10
WN = ("q", "v", "k", "o")
SPLIT_AT = {(-1, 1): (0, "q", 0), (-1, 2): (0, "q", 1), (-1, 3): (0, "v", 0), (-1, 4): (0, "v", 1),
            (-1, 5): (0, "k", 0), (-1, 6): (0, "k", 1), (-1, 13): (0, "o", 0), (-1, 14): (0, "o", 1),
            (14, 9): (1, "q", 0), (14, 10): (1, "q", 1), (15, 4): (1, "v", 0), (15, 5): (1, "v", 1),
            (15, 7): (1, "k", 0), (15, 8): (1, "k", 1), (16, 9): (1, "o", 0), (16, 10): (1, "o", 1)}
FIRST_SPLIT_AT = {(NS - 2, 9): 0, (NS - 2, 10): 1}
FIRST_STATS_AT, FIRST_AGGR_AT = {(NS - 2, 12): 0, (NS - 2, 13): 1, (NS - 2, 14): 2, (NS - 2, 15): 3}, (NS - 1, 0)
FIRST_SCALE_AT = {(NS - 1, 1): (0, 1), (NS - 1, 2): (2, 3)}
PARTS = 3


class Slot:

    def __init__(self, at, pair=None):
        self.at, self.odd = at, at % 2
        self.pair = at // 2 if pair is None else pair
        self.n = 2 * self.pair + self.odd
        self.layer = min(max(at // B, 0), 1)
        self.b = self.n - B * self.layer

    def step(self, k):
        at = self.at + k
        return Slot(at, self.pair + (self.at % 2 + k) // 2)

    @property
    def real(self):
        return 0 <= self.at < NS


def at_least(eng, sem, value):
    if not isinstance(value, int) or value > 0:
        eng.wait_ge(sem, value)


def slots(eng, body):
    for at in (-2, -1, 0):
        body(Slot(at))
    with eng.Fori(0, 6) as i:
        body(Slot(1, i))
        body(Slot(2, i + 1))
    for at in (13, 14, 15, 16):
        body(Slot(at))
    with eng.Fori(0, 6) as i:
        body(Slot(17, i + 8))
        body(Slot(18, i + 9))
    for at in (29, 30, 31, 32):
        body(Slot(at))


def chunks_at(n, h):
    if not n.real:
        return ()
    if n.at == 0:
        return range(C) if T_AT.get(h) == 0 else ()
    return (T_AT[h],) if h in T_AT else ()


def work_bank(s, i):
    return (i + len(WORK) * s.odd) % 2


def ended(s, h):
    for i, (kind, k, ahead, steps) in enumerate(WORK):
        if max(steps) == h and s.step(ahead).real:
            yield work_bank(s, i), kind, k, s.step(ahead)


def w_split(layer, name):
    return 2 * (4 * layer + WN.index(name) + 1)


def row3(ap, b):
    return ap[bass.ds(b, 1), :, :].rearrange("o p d -> (o p) d")


def attention_layers(nc, a, hidden, mlp_start):
    with ExitStack() as ctx:
        def sb(name, shape, dt=F32):
            return ctx.enter_context(nc.sbuf_tensor(name, shape, dt))

        def ps(name, shape):
            return ctx.enter_context(nc.psum_tensor(name, shape, F32))

        def sem(name):
            return ctx.enter_context(nc.semaphore(name))

        w_hi, w_lo, x_out, x_stored = mlp_start.w_hi, mlp_start.w_lo, mlp_start.x_out, mlp_start.x_stored
        cT_hi, cT_lo, c32 = mlp_start.turned_hi, mlp_start.turned_lo, mlp_start.turned32
        w_stage = [half for both in (mlp_start.stage, mlp_start.y_and_stage[:, :, :].rearrange("p (i c) n -> p i c n", i=2))
                   for half in (both[:, 0, :, :], both[:, 1, :, :])]
        ident, eps, minus_half = mlp_start.ident, mlp_start.eps, mlp_start.minus_half
        ctx_g, ctx_b = sb("ctx_g", [128, C]), sb("ctx_b", [128, C])
        ln1_g, ln1_b = sb("ln1_g", [T, D]), sb("ln1_b", [T, D])
        q_bias, o_bias = sb("q_bias", [T, D]), sb("o_bias", [T, D])
        k_bias, v_bias = sb("k_bias", [128, C]), sb("v_bias", [128, C])
        gate = sb("gate", [128, 1])
        ctx_in = sb("ctx_in", [KR, KT, D])
        x_in = sb("x_in", [T, D])
        ctx_st, ctx_mv = sb("ctx_st", [KR, KT, 6]), sb("ctx_mv", [KR, KT, 2])
        ctx_rs, ctx_nm = sb("ctx_rs", [KR, KT]), sb("ctx_nm", [KR, KT])
        x_st, x_mv, x_rs = sb("x_st", [T, 6]), sb("x_mv", [T, 2]), sb("x_rs", [T, 1])
        ctx_ve, x_ve = sb("ctx_ve", [KR, KT]), sb("x_ve", [T, 1])
        xT_hi, xT_lo = sb("xT_hi", [128, C, T], F32R), sb("xT_lo", [128, C, T], F32R)
        q32 = sb("q32", [T, D])
        qT_hi, qT_lo = sb("qT_hi", [128, G, T], F32R), sb("qT_lo", [128, G, T], F32R)
        kT_hi, kT_lo = sb("kT_hi", [128, G, SE], F32R), sb("kT_lo", [128, G, SE], F32R)
        q_st = sb("q_st", [96, 2, GH, G, T], F32R)
        k_st = sb("k_st", [96, H, SE], F32R)
        v32 = sb("v32", [KR, 2, KT, D])
        mask8 = sb("mask8", [T, S], U8)
        minus_one, big = sb("minus_one", [T, 1]), sb("big", [T, 1])
        mask_add = sb("mask_add", [T, 2, S])
        p = sb("p", [T, 4, SP])
        p_min, p_sum, p_rec = sb("p_min", [T, 4]), sb("p_sum", [T, 4]), sb("p_rec", [T, 4])
        pT = sb("pT", [KR, 2, KT, GH, T])
        ao32 = sb("ao32", [128, G, T])
        ao_hi, ao_lo = sb("ao_hi", [128, G, T], F32R), sb("ao_lo", [128, G, T], F32R)
        res = sb("res", [T, D])

        work = ps("work", [128, 2, 512])
        side = ps("side", [128, 512])
        scores = ps("scores", [128, 2, 512])
        turned = ps("turned", [128, 2, 512])
        mixed = ps("mixed", [128, 512])

        def chunk_bank(n, c):
            return side if n.at != 0 else (side, mixed, scores[:, 0, :], scores[:, 1, :])[c]

        consts1_in = sem("consts1_in")
        consts_in, w_in = sem("consts_in"), [sem(f"w_in{i}") for i in range(4)]
        ctx_loaded, x_loaded, mask_loaded, res_loaded = (
            sem("ctx_loaded"), sem("x_loaded"), sem("mask_loaded"), sem("res_loaded"))
        q_stacked = sem("q_stacked")
        k_stacked = [sem(f"k_stacked{g}") for g in range(G)]
        gate_done, w_hi_done = sem("gate_done"), sem("w_hi_done")
        ctx_scaled = sem("ctx_scaled")
        cT_hi_done, xT_hi_done, qT_hi_done, kT_hi_done = (
            sem("cT_hi_done"), sem("xT_hi_done"), sem("qT_hi_done"), sem("kT_hi_done"))
        v_done, exp_done, pT_done, ao_hi_done = (
            sem("v_done"), sem("exp_done"), sem("pT_done"), sem("ao_hi_done"))
        w_lo_done = sem("w_lo_done")
        ctx_stats, ctx_aggr, ctx_rstd, ctx_shift = (
            sem("ctx_stats"), sem("ctx_aggr"), sem("ctx_rstd"), sem("ctx_shift"))
        x_stats, x_aggr, x_rstd, x_scaled = (
            sem("x_stats"), sem("x_aggr"), sem("x_rstd"), sem("x_scaled"))
        c32_done = sem("c32_done")
        cT_done, xT_done, q_done, qT_done, kT_done = (
            sem("cT_done"), sem("xT_done"), sem("q_done"), sem("qT_done"), sem("kT_done"))
        masked, rec_done, p_done = sem("masked"), sem("rec_done"), sem("p_done")
        ao32_done, ao_done, o_done = sem("ao32_done"), sem("ao_done"), sem("o_done")
        pads_done, mask_less_one, mask_lowest, mask_ready = (
            sem("pads_done"), sem("mask_less_one"), sem("mask_lowest"), sem("mask_ready"))
        ctx_var, x_var = sem("ctx_var"), sem("x_var")
        x_weighted, x_ready, res_ready = sem("x_weighted"), sem("x_ready"), sem("res_ready")
        cT_made, xT_made, q_made, qT_made, k_made, v_made, o_made = (
            sem("cT_made"), sem("xT_made"), sem("q_made"), sem("qT_made"), sem("k_made"),
            sem("v_made"), sem("o_made"))
        s_made, pT_made, pv_made = sem("s_made"), sem("pT_made"), sem("pv_made")

        block = ctx.enter_context(nc.Block())

        @block.sync
        def _(sp):
            def constants():
                for dst, src in ((ctx_g, a["g0"]), (ctx_b, a["b0"]), (k_bias, a["k_b"]), (v_bias, a["v_b"])):
                    sp.dma_start(dst[:, :], src).then_inc(consts_in, 16)
                sp.dma_start(gate[:, :], a["gate"].rearrange("(o d) -> o d", o=1).broadcast_to([128, 1])).then_inc(consts_in, 16)

            def constants1():
                for dst, src in ((ln1_g, a["ln1_w"]), (ln1_b, a["ln1_b"]), (q_bias, a["q_b"]), (o_bias, a["cproj_b"])):
                    sp.dma_start(dst[:, :], src.rearrange("(o d) -> o d", o=1).broadcast_to([T, D])).then_inc(consts1_in, 16)

            def weights(layer, name):
                src = a[f"w{layer}{name}"].rearrange("(j c p) n -> j p c n", j=2, p=128)
                for j in range(2):
                    i = w_split(layer, name) - 2 + j
                    at_least(sp, w_lo_done, i - 3)
                    sp.dma_start(w_stage[i % 4], src[j, :, :, :]).then_inc(w_in[i % 4], 16)

            def stack_k(y, g):
                at_least(sp, kT_done, G * y.n + g + 1)
                for part, src in enumerate((kT_hi, kT_hi, kT_lo)):
                    dst = k_st[HD * part:HD * (part + 1), GH * g:GH * (g + 1), :]
                    sp.dma_start(dst.bitcast(F32), src[:, g, :].bitcast(F32)).then_inc(k_stacked[g], 16)

            def body(s):
                n, m, z = s.step(1), s.step(2), s.step(-1)
                if s.at == 14:
                    weights(1, "q")
                if m.real:
                    at_least(sp, xT_made, n.n + 1)
                    if m.layer == 1:
                        at_least(sp, x_stored, 16 * (m.b + 1))
                    sp.dma_start(x_in[:, :], row3(a["x"] if m.layer == 0 else hidden, m.b)).then_inc(x_loaded, 16)
                if s.at == -1:
                    weights(0, "k")
                if s.real:
                    stack_k(s, G - 1)
                if s.at == 15:
                    weights(1, "k")
                if n.real:
                    at_least(sp, mask_ready, n.n)
                if m.real:
                    at_least(sp, cT_made, C * n.n + C)
                    sp.dma_start(ctx_in[:, :, :], a["ctx"][bass.ds(m.b, 1), :, :, :].rearrange("o k p d -> p (o k) d")).then_inc(ctx_loaded, 16)
                if n.real:
                    sp.dma_start(mask8[:, :], a["mask"][bass.ds(n.b, 1), :].broadcast_to([T, S])).then_inc(mask_loaded, 16)
                if s.at == -2:
                    weights(0, "q")
                    constants()
                    weights(0, "v")
                if s.at == -1:
                    weights(0, "o")
                    constants1()
                if s.at == 29:
                    for i in (0, 1):
                        mlp_start.load_piece(sp, a, i, w_stage)
                    for dst, src in ((mlp_start.ln_g, a["ln2_w"]), (mlp_start.ln_b, a["ln2_b"]), (mlp_start.f_bias, a["fc_b"]), (mlp_start.p_bias, a["proj_b"])):
                        sp.dma_start(dst[:, :], src).then_inc(mlp_start.consts_in, 16)
                    sp.wait_ge(x_stored, 16 * (B + MG))
                    mlp_start.load_rows(sp, hidden, 0)
                if s.at == 14:
                    weights(1, "v")
                if s.at == 15:
                    weights(1, "o")
                if s.at == NS - 1:
                    for i in (2, 3):
                        mlp_start.load_piece(sp, a, i, w_stage)
                if z.real:
                    at_least(sp, o_done, z.n + 1)
                    sp.dma_start(row3(hidden, z.b), x_out[:, :]).then_inc(x_stored, 16)
                if s.real:
                    sp.dma_start(res[:, :], row3(a["x"] if s.layer == 0 else hidden, s.b)).then_inc(res_loaded, 16)
                if n.real:
                    at_least(sp, qT_done, n.n + 1)
                    for part, src in enumerate((qT_hi, qT_lo, qT_hi)):
                        sp.dma_start(q_st[HD * part:HD * (part + 1), n.odd, :, :, :].bitcast(F32), src[:, :, :].bitcast(F32)).then_inc(q_stacked, 16)
                    for g in range(G - 1):
                        stack_k(n, g)

            slots(sp, body)

        @block.gpsimd
        def _(pool):
            pool.memset(p[:, :, S:SP], 0.0).then_inc(pads_done, 1)
            pool.memset(minus_one[:, :], -1.0).then_inc(pads_done, 1)
            pool.memset(big[:, :], BIG).then_inc(pads_done, 1)
            pool.memset(eps[:, :], EPS).then_inc(pads_done, 1)
            pool.memset(minus_half[:, :], -0.5).then_inc(pads_done, 1)
            pool.wait_ge(pads_done, 5)

            def body(s):
                n, m, z = s.step(1), s.step(2), s.step(-1)
                if s.at == 13:
                    pool.wait_ge(consts1_in, 16 * 4)
                if n.real and n.layer == 0:
                    for c in range(C):
                        pool.wait_ge(c32_done, C * n.n + c + 1)
                        pool.tensor_tensor(cT_lo[:, c, 0:SP], c32[:, c % 2, 0:SP], cT_hi[:, c, 0:SP].bitcast(F32), ALU.subtract).then_inc(cT_done, 1)
                if n.real:
                    pool.wait_ge(mask_loaded, 16 * (n.n + 1))
                    at_least(pool, masked, H * s.n)
                    half = mask_add[:, n.odd, :]
                    pool.tensor_tensor(half, mask8[:, :], minus_one[:, :].broadcast_to([T, S]), ALU.add).then_inc(mask_less_one, 1)
                    pool.wait_ge(mask_less_one, n.n + 1)
                    lowest = pool.tensor_tensor(half, half, big[:, :].broadcast_to([T, S]), ALU.mult)
                    lowest.then_inc(mask_lowest if n.layer == 0 else mask_ready, 1)
                    if n.layer == 0:
                        pool.wait_ge(mask_lowest, n.n + 1)
                        pool.tensor_tensor(half, half, half, ALU.add).then_inc(mask_ready, 1)
                if m.real and m.layer == 0:
                    pool.wait_ge(ctx_aggr, KT * (m.n + 1))
                    pool.tensor_tensor(ctx_ve[:, :], ctx_mv[:, :, 1], eps[0:KR, :].broadcast_to([KR, KT]), ALU.add).then_inc(ctx_var, 1)
                    pool.wait_ge(ctx_var, m.n + 1)
                    pool.tensor_tensor(ctx_rs[:, :], ctx_ve[:, :], minus_half[0:KR, :].broadcast_to([KR, KT]), ALU.pow).then_inc(ctx_rstd, 1)
                if m.real and m.layer == 1:
                    pool.wait_ge(x_aggr, m.b + 1)
                    pool.tensor_tensor(x_ve[:, :], x_mv[:, 1:2], eps[0:T, :], ALU.add).then_inc(x_var, 1)
                    pool.wait_ge(x_var, m.b + 1)
                    pool.tensor_tensor(x_rs[:, :], x_ve[:, :], minus_half[0:T, :], ALU.pow).then_inc(x_rstd, 1)
                    pool.wait_ge(x_scaled, m.b + 1)
                    pool.tensor_tensor(x_in[:, :], x_in[:, :], ln1_g[:, :], ALU.mult).then_inc(x_weighted, 1)
                    pool.wait_ge(x_weighted, m.b + 1)
                    pool.tensor_tensor(x_in[:, :], x_in[:, :], ln1_b[:, :], ALU.add).then_inc(x_ready, 1)
                if s.at == NS - 2:
                    mlp_start.row_rstd(pool, 0)
                if s.at == NS - 1:
                    for c in range(C):
                        mlp_start.turned_to_lo(pool, 0, c)
                if s.real and s.layer == 1:
                    pool.wait_ge(res_loaded, 16 * (s.n + 1))
                    pool.tensor_tensor(res[:, :], res[:, :], o_bias[:, :], ALU.add).then_inc(res_ready, 1)

            slots(pool, body)

        @block.scalar
        def _(act):
            def split_weights(layer, name, j):
                i = w_split(layer, name) - 2 + j
                if layer:
                    act.wait_ge({"q": q_made, "k": k_made, "v": v_made, "o": o_made}[name], B * {"q": 1, "k": G, "v": KT, "o": 1}[name])
                act.wait_ge(w_in[i % 4], 16 * (i // 4 + 1))
                act.copy(w_hi[name][:, j * C // 2:(j + 1) * C // 2, :], w_stage[i % 4]).then_inc(w_hi_done, 1)

            def context_affine(y, k):
                act.wait_ge(ctx_shift, y.n + 1)
                act.activation(ctx_in[:, k, :], ctx_in[:, k, :], ACT.Identity, bias=ctx_nm[:, k:k + 1], scale=ctx_rs[:, k:k + 1]).then_inc(ctx_scaled, 1)

            def body(s):
                n, m, z = s.step(1), s.step(2), s.step(-1)
                for h in range(H):
                    if s.real:
                        act.wait_ge(masked, H * s.n + h + 1)
                        act.activation(p[:, h % 4, 0:S], p[:, h % 4, 0:S], ACT.Exp, bias=p_min[:, h % 4:h % 4 + 1], scale=-1.0,
                                       accum_out=p_sum[:, h % 4:h % 4 + 1]).then_inc(exp_done, 1)
                    if z.real and h == AO_AT + 1:
                        act.wait_ge(ao32_done, z.n + 1)
                        at_least(act, o_made, z.n)
                        act.copy(ao_hi[:, :, :], ao32[:, :, :]).then_inc(ao_hi_done, 1)
                    for bank, kind, k, y in ended(s, h):
                        if kind == "K":
                            act.wait_ge(k_made, G * y.n + k + 1)
                            at_least(act, k_stacked[k], 16 * PARTS * y.n)
                            src = work[:, bank, 0:SE]
                            if y.layer == 0:
                                act.copy(kT_hi[:, k, :], src).then_inc(kT_hi_done, 1)
                            else:
                                act.activation(kT_hi[:, k, :], src, ACT.Identity, bias=k_bias[:, k:k + 1]).then_inc(kT_hi_done, 1)
                        if kind == "V":
                            act.wait_ge(v_made, KT * y.n + k + 1)
                            at_least(act, pv_made, G * (y.n - 1))
                            act.copy(v32[:, y.odd, k, :], work[0:KR, bank, :]).then_inc(v_done, 1)
                    if n.real and h == XT_AT:
                        act.wait_ge(xT_made, n.n + 1)
                        at_least(act, q_made, n.n)
                        act.copy(xT_hi[:, :, :], side[:, 0:C * T].rearrange("p (c t) -> p c t", c=C)).then_inc(xT_hi_done, 1)
                    if s.at == -1 and h == XT_AT:
                        act.wait_ge(consts_in, 16 * 5)
                        act.activation(gate[:, :], gate[:, :], ACT.Tanh).then_inc(gate_done, 1)
                    if s.at == NS - 1 and h in T_AT:
                        if T_AT[h] == 0:
                            act.wait_ge(k_made, G * NS)
                            act.wait_ge(v_made, KT * NS)
                            act.wait_ge(mlp_start.consts_in, 16 * 4)
                        mlp_start.turned_to_hi(act, side, 0, T_AT[h])
                    for c in chunks_at(n, h):
                        act.wait_ge(cT_made, C * n.n + c + 1)
                        if c == 0:
                            at_least(act, k_made, G * n.n)
                            at_least(act, v_made, KT * n.n)
                        if n.layer == 0:
                            act.activation(cT_hi[:, c, 0:SP], chunk_bank(n, c)[:, 0:SP], ACT.Identity, bias=ctx_b[:, c:c + 1], scale=ctx_g[:, c:c + 1]).then_inc(cT_hi_done, 1)
                        else:
                            act.copy(cT_hi[:, c, 0:SP], chunk_bank(n, c)[:, 0:SP]).then_inc(cT_hi_done, 1)
                    if n.real and h == QT_AT:
                        act.wait_ge(qT_made, n.n + 1)
                        at_least(act, q_stacked, 16 * PARTS * n.n)
                        act.copy(qT_hi[:, :, :], side[:, 0:G * T].rearrange("p (c t) -> p c t", c=G)).then_inc(qT_hi_done, 1)
                    y, hh = (s, h - LAG) if h >= LAG else (z, h - LAG + H)
                    if y.real:
                        act.wait_ge(pT_made, H * y.n + hh + 1)
                        g, j = hh // GH, hh % GH
                        if j == 0:
                            at_least(act, pv_made, G * y.n + g - 1)
                        act.copy(pT[:, g % 2, :, j, :], turned[0:KR, hh % 2, 0:KT * T].rearrange("p (k t) -> p k t", k=KT)).then_inc(pT_done, 1)
                    if h in CTX_SCALE_AT:
                        k, ahead = CTX_SCALE_AT[h]
                        if s.step(ahead).real and s.step(ahead).layer == 0:
                            context_affine(s.step(ahead), k)
                    if (s.at, h) in FIRST_SPLIT_AT:
                        act.wait_ge(q_made, NS)
                        mlp_start.split_hi(act, FIRST_SPLIT_AT[s.at, h], w_hi["q"], w_stage)
                    if (s.at, h) in SPLIT_AT:
                        split_weights(*SPLIT_AT[s.at, h])
                    if s.at == NS and h == O_END:
                        break

            slots(act, body)

        @block.vector
        def _(dve):
            dve.wait_ge(pads_done, 5)

            def split_weights(layer, name, j):
                i = w_split(layer, name) - 2 + j
                dve.wait_ge(w_hi_done, i + 1)
                c = slice(j * C // 2, (j + 1) * C // 2)
                dve.tensor_tensor(w_lo[name][:, c, :], w_stage[i % 4], w_hi[name][:, c, :].bitcast(F32), ALU.subtract).then_inc(w_lo_done, 1)

            def body(s):
                n, m, z = s.step(1), s.step(2), s.step(-1)
                if s.at == -1:
                    dve.wait_ge(gate_done, 1)
                for h in range(H):
                    y, hh = (s, h - 1) if h else (z, H - 1)
                    if s.real:
                        if h == 0:
                            dve.wait_ge(mask_ready, s.n + 1)
                        dve.wait_ge(s_made, H * s.n + h + 1)
                        at_least(dve, pT_made, H * s.n + h - 3)
                    if m.real and m.layer == 0 and h == CTX_AGGR_AT:
                        dve.wait_ge(ctx_stats, KT * (m.n + 1))
                    if m.real and m.layer == 1 and h == X_AGGR_AT:
                        dve.wait_ge(x_stats, m.b + 1)
                    if y.real:
                        dve.wait_ge(exp_done, H * y.n + hh + 1)
                        dve.reciprocal(p_rec[:, hh % 4:hh % 4 + 1], p_sum[:, hh % 4:hh % 4 + 1]).then_inc(rec_done, 1)
                    if s.real:
                        dve.tensor_tensor_reduce(out=p[:, h % 4, 0:S], in0=scores[0:T, h % 2, 0:S], in1=mask_add[:, s.odd, :],
                                                 scale=-SCALE, scalar=BIG, op0=ALU.add, op1=ALU.min,
                                                 accum_out=p_min[:, h % 4:h % 4 + 1]).then_inc(masked, 1)
                    if s.at == NS - 1 and h - 1 in T_AT:
                        mlp_start.turned_to_32(dve, side, 0, T_AT[h - 1])
                    for c in chunks_at(n, h - 1):
                        dve.wait_ge(cT_hi_done, C * n.n + c + 1)
                        if n.layer == 0:
                            if c >= 2:
                                dve.wait_ge(cT_done, C * n.n + c - 1)
                            dve.tensor_scalar(c32[:, c % 2, 0:SP], chunk_bank(n, c)[:, 0:SP], ctx_g[:, c:c + 1], ctx_b[:, c:c + 1], ALU.mult, ALU.add).then_inc(c32_done, 1)
                        else:
                            dve.tensor_tensor(cT_lo[:, c, 0:SP], chunk_bank(n, c)[:, 0:SP], cT_hi[:, c, 0:SP].bitcast(F32), ALU.subtract).then_inc(cT_done, 1)
                    if n.real and h == QT_AT + 1:
                        dve.wait_ge(qT_hi_done, n.n + 1)
                        dve.tensor_tensor(qT_lo[:, :, :], side[:, 0:G * T].rearrange("p (c t) -> p c t", c=G), qT_hi[:, :, :].bitcast(F32), ALU.subtract).then_inc(qT_done, 1)
                    for bank, kind, k, v in ended(*((s, h - 1) if h else (z, H - 1))):
                        if kind == "K":
                            dve.wait_ge(kT_hi_done, G * v.n + k + 1)
                            src = work[:, bank, 0:SE]
                            hi = kT_hi[:, k, :].bitcast(F32)
                            if v.layer == 0:
                                dve.tensor_tensor(kT_lo[:, k, :], src, hi, ALU.subtract).then_inc(kT_done, 1)
                            else:
                                dve.scalar_tensor_tensor(kT_lo[:, k, :], src, k_bias[:, k:k + 1], hi, ALU.add, ALU.subtract).then_inc(kT_done, 1)
                        if kind == "Q":
                            dve.wait_ge(q_made, v.n + 1)
                            at_least(dve, qT_made, v.n)
                            if v.layer == 0:
                                dve.tensor_copy(q32[:, :], work[0:T, bank, :]).then_inc(q_done, 1)
                            else:
                                dve.tensor_tensor(q32[:, :], work[0:T, bank, :], q_bias[:, :], ALU.add).then_inc(q_done, 1)
                        if kind == "O":
                            dve.wait_ge(o_made, v.n + 1)
                            at_least(dve, x_stored, 16 * v.n)
                            if v.layer == 0:
                                dve.wait_ge(res_loaded, 16 * (v.n + 1))
                                dve.scalar_tensor_tensor(x_out[:, :], work[0:T, bank, :], gate[0:T, :], res[:, :], ALU.mult, ALU.add).then_inc(o_done, 1)
                            else:
                                dve.wait_ge(res_ready, v.b + 1)
                                dve.tensor_tensor(x_out[:, :], work[0:T, bank, :], res[:, :], ALU.add).then_inc(o_done, 1)
                    if n.real and h == XT_AT + 1:
                        dve.wait_ge(xT_hi_done, n.n + 1)
                        dve.tensor_tensor(xT_lo[:, :, :], side[:, 0:C * T].rearrange("p (c t) -> p c t", c=C), xT_hi[:, :, :].bitcast(F32), ALU.subtract).then_inc(xT_done, 1)
                    if z.real and h == AO_AT + 1:
                        dve.wait_ge(pv_made, G * z.n + G)
                        src = mixed[:, 0:G * T].rearrange("p (g t) -> p g t", g=G)
                        if z.layer == 0:
                            dve.tensor_copy(ao32[:, :, :], src).then_inc(ao32_done, 1)
                        else:
                            dve.tensor_tensor(ao32[:, :, :], src, v_bias[:, :].unsqueeze(2).broadcast_to([128, G, T]), ALU.add).then_inc(ao32_done, 1)
                    if z.real and h == AO_AT + 2:
                        dve.wait_ge(ao_hi_done, z.n + 1)
                        dve.tensor_tensor(ao_lo[:, :, :], ao32[:, :, :], ao_hi[:, :, :].bitcast(F32), ALU.subtract).then_inc(ao_done, 1)
                    if y.real:
                        dve.wait_ge(rec_done, H * y.n + hh + 1)
                        dve.tensor_scalar(p[:, hh % 4, 0:S], p[:, hh % 4, 0:S], p_rec[:, hh % 4:hh % 4 + 1], None, ALU.mult).then_inc(p_done, 1)
                    if m.real and m.layer == 0:
                        if h in CTX_STATS_AT:
                            k = CTX_STATS_AT[h]
                            dve.wait_ge(ctx_loaded, 16 * (m.n + 1))
                            dve.bn_stats(ctx_st[:, k, :], ctx_in[:, k, :]).then_inc(ctx_stats, 1)
                        if h == CTX_AGGR_AT:
                            for k in range(KT):
                                dve.bn_aggr(ctx_mv[:, k, :], ctx_st[:, k, :]).then_inc(ctx_aggr, 1)
                        if h == CTX_SHIFT_AT:
                            dve.wait_ge(ctx_rstd, m.n + 1)
                            dve.scalar_tensor_tensor(ctx_nm[:, :], ctx_mv[:, :, 0], -1.0, ctx_rs[:, :], ALU.mult, ALU.mult).then_inc(ctx_shift, 1)
                    if m.real and m.layer == 1:
                        if h == X_STATS_AT:
                            dve.wait_ge(x_loaded, 16 * (m.n + 1))
                            dve.bn_stats(x_st[:, :], x_in[:, :]).then_inc(x_stats, 1)
                        if h == X_AGGR_AT:
                            dve.bn_aggr(x_mv[:, :], x_st[:, :]).then_inc(x_aggr, 1)
                        if h == X_SCALE_AT:
                            dve.wait_ge(x_rstd, m.b + 1)
                            dve.tensor_scalar(x_in[:, :], x_in[:, :], x_mv[:, 0:1], x_rs[:, 0:1], ALU.subtract, ALU.mult).then_inc(x_scaled, 1)
                    if (s.at, h - 1) in SPLIT_AT:
                        split_weights(*SPLIT_AT[s.at, h - 1])
                    if (s.at, h - 1) in FIRST_SPLIT_AT:
                        mlp_start.split_lo(dve, FIRST_SPLIT_AT[s.at, h - 1], w_hi["q"], w_lo["q"], w_stage)
                    if (s.at, h) in FIRST_STATS_AT:
                        mlp_start.row_stats(dve, 0, FIRST_STATS_AT[s.at, h])
                    if (s.at, h) == FIRST_AGGR_AT:
                        mlp_start.row_aggr(dve, 0)
                    for i in FIRST_SCALE_AT.get((s.at, h), ()):
                        mlp_start.row_scale(dve, 0, i)
                    if s.at == NS and h == O_END + 1:
                        break

            slots(dve, body)

        @block.tensor
        def _(pe):
            pe.wait_ge(mlp_start.ident_ready, 2)

            def pieces(out, pairs, first, last, chunk_ready=None):
                todo = [(x, y) for (x_hi, x_lo, y_hi, y_lo) in pairs for (x, y) in ((x_hi, y_hi), (x_hi, y_lo), (x_lo, y_hi))]
                for i in range(first, last):
                    if chunk_ready and i % 3 == 0:
                        chunk_ready(i // 3)
                    made = pe.matmul(out, *todo[i], start=i == 0, stop=i == len(todo) - 1)
                return made

            def bank_free(s, i):
                while s.at >= -1:
                    i -= 2
                    if i < 0:
                        s, i = s.step(-1), i + len(WORK)
                    kind, k, ahead, _ = WORK[i]
                    y = s.step(ahead)
                    if y.real:
                        done, per = {"K": (kT_done, G), "V": (v_done, KT), "Q": (q_done, 1), "O": (o_done, 1)}[kind]
                        pe.wait_ge(done, per * y.n + k + 1)
                        return

            def work_item(s, i, h):
                kind, k, ahead, steps = WORK[i]
                y = s.step(ahead)
                if not y.real or h not in steps:
                    return
                if h == min(steps):
                    bank_free(s, i)
                    if kind == "Q":
                        pe.wait_ge(xT_done, y.n + 1)
                    elif kind == "O":
                        pe.wait_ge(ao_done, y.n + 1)
                    pe.wait_ge(w_lo_done, w_split(y.layer, kind.lower()))
                bank = work[:, work_bank(s, i), :]
                if kind == "Q":
                    out, made = bank[0:T, :], q_made
                    pairs = [(xT_hi[:, c, :], xT_lo[:, c, :], w_hi["q"][:, c, :], w_lo["q"][:, c, :]) for c in range(C)]
                elif kind == "K":
                    out, made, w = bank[:, 0:SE], k_made, slice(k * 128, (k + 1) * 128)
                    pairs = [(w_hi["k"][:, c, w], w_lo["k"][:, c, w], cT_hi[:, c, 0:SE], cT_lo[:, c, 0:SE]) for c in range(C)]
                elif kind == "V":
                    out, made, r = bank[0:KR, :], v_made, slice(k * KR, (k + 1) * KR)
                    pairs = [(cT_hi[:, c, r], cT_lo[:, c, r], w_hi["v"][:, c, :], w_lo["v"][:, c, :]) for c in range(C)]
                else:
                    out, made = bank[0:T, :], o_made
                    pairs = [(ao_hi[:, c, :], ao_lo[:, c, :], w_hi["o"][:, c, :], w_lo["o"][:, c, :]) for c in range(C)]
                def context_ready(c):
                    pe.wait_ge(cT_done, C * y.n + c + 1)

                first = sum(count for step, count in steps.items() if step < h)
                last = pieces(out, pairs, first, first + steps[h], context_ready if i == FIRST_CONTEXT_USE else None)
                if h == max(steps):
                    last.then_inc(made, 1)

            def body(s):
                n, z = s.step(1), s.step(-1)
                for h in range(H):
                    if s.real:
                        if h == 0:
                            pe.wait_ge(q_stacked, 16 * PARTS * (s.n + 1))
                        if h % GH == 0:
                            pe.wait_ge(k_stacked[h // GH], 16 * PARTS * (s.n + 1))
                        at_least(pe, masked, H * s.n + h - 1)
                        pe.matmul(scores[0:T, h % 2, 0:SE], q_st[:, s.odd, h % GH, h // GH, :], k_st[:, h, :], start=True, stop=True).then_inc(s_made, 1)
                    for i in range(len(WORK)):
                        work_item(s, i, h)
                    if h in PV_AT:
                        g = PV_AT[h]
                        y = z if g == G - 1 else s
                        if y.real:
                            pe.wait_ge(pT_done, H * y.n + GH * (g + 1))
                            if g == 0:
                                pe.wait_ge(v_done, KT * (y.n + 1))
                                at_least(pe, ao32_done, y.n)
                            for k in range(KT):
                                for j in range(GH):
                                    hd = (GH * g + j) * HD
                                    last = pe.matmul(mixed[32 * j:32 * j + 32, g * T:(g + 1) * T], v32[:, y.odd, k, hd:hd + HD], pT[:, g % 2, k, j, :],
                                                     start=k == 0, stop=k == KT - 1)
                            last.then_inc(pv_made, 1)
                    if n.real and h == XT_AT:
                        if n.layer == 0:
                            pe.wait_ge(x_loaded, 16 * (n.n + 1))
                        else:
                            pe.wait_ge(x_ready, n.b + 1)
                        at_least(pe, qT_done, n.n)
                        for c in range(C):
                            last = pe.transpose(side[:, c * T:(c + 1) * T], x_in[:, c * 128:(c + 1) * 128], ident[0:T, 0:T])
                        last.then_inc(xT_made, 1)
                    if s.at == NS - 1 and h in T_AT:
                        if T_AT[h] == 0:
                            pe.wait_ge(qT_done, NS)
                        else:
                            pe.wait_ge(mlp_start.y32_done, T_AT[h])
                        mlp_start.turn(pe, side, 0, T_AT[h])
                    for c in chunks_at(n, h):
                        if c == 0:
                            if n.layer == 0:
                                pe.wait_ge(ctx_scaled, KT * (n.n + 1))
                            else:
                                pe.wait_ge(ctx_loaded, 16 * (n.n + 1))
                            pe.wait_ge(xT_done, n.n + 1)
                        elif n.at != 0:
                            pe.wait_ge(c32_done if n.layer == 0 else cT_done, C * n.n + c)
                        for k in range(KT):
                            last = pe.transpose(chunk_bank(n, c)[:, k * KR:(k + 1) * KR], ctx_in[:, k, c * 128:(c + 1) * 128], ident[0:KR, 0:KR])
                        last.then_inc(cT_made, 1)
                    if n.real and h == QT_AT:
                        pe.wait_ge(q_done, n.n + 1)
                        pe.wait_ge(c32_done if n.layer == 0 else cT_done, C * n.n + C)
                        for g in range(G):
                            last = pe.transpose(side[:, g * T:(g + 1) * T], q32[:, g * 128:(g + 1) * 128], ident[0:T, 0:T])
                        last.then_inc(qT_made, 1)
                    y, hh = (s, h - LAG) if h >= LAG else (z, h - LAG + H)
                    if y.real:
                        pe.wait_ge(p_done, H * y.n + hh + 1)
                        at_least(pe, pT_done, H * y.n + hh - 1)
                        for k in range(KT):
                            last = pe.transpose(turned[0:KR, hh % 2, k * T:(k + 1) * T], p[:, hh % 4, k * KR:(k + 1) * KR], ident[0:T, 0:T])
                        last.then_inc(pT_made, 1)
                    if s.at == NS and h == O_END:
                        break

            slots(pe, body)


class Mlp:

    def __init__(self, nc, ctx):
        def sb(name, shape, dt=F32):
            return ctx.enter_context(nc.sbuf_tensor(name, shape, dt))

        def sem(name):
            return ctx.enter_context(nc.semaphore(name))

        self.ident = sb("ident", [128, 128])
        self.w_hi = {x: sb(f"w{x}_hi", [128, C, D], F32R) for x in WN}
        self.w_lo = {x: sb(f"w{x}_lo", [128, C, D], F32R) for x in WN}
        self.stage = sb("stage", [128, 2, C // 2, D])
        self.y_and_stage = sb("y", [128, MG, D])
        self.y = self.y_and_stage[0:T, :, :]
        self.turned_hi, self.turned_lo = sb("turned_hi", [128, C, MG * T], F32R), sb("turned_lo", [128, C, MG * T], F32R)
        self.turned32 = sb("turned32", [128, 2, MG * T])
        self.x_out = sb("x_out", [T, D])
        self.ln_g, self.ln_b, self.f_bias = sb("ln2_g", [128, C]), sb("ln2_b", [128, C]), sb("f_bias", [128, FC])
        self.p_bias = sb("p_bias", [128, C])
        self.st, self.mv = sb("mlp_st", [T, MG, 6]), sb("mlp_mv", [T, MG, 2])
        self.ve, self.rs, self.after_stats = sb("mlp_ve", [T, MG]), sb("mlp_rs", [T, MG]), sb("after_stats", [T, 1])
        self.eps, self.minus_half = sb("eps", [128, 1]), sb("minus_half", [128, 1])
        self.ident_ready, self.consts_in, self.x_stored = sem("ident_ready"), sem("mlp_consts_in"), sem("x_stored")
        self.w_in = [sem(f"mlp_w_in{i}") for i in range(4)]
        self.w_hi_done, self.w_lo_done = sem("mlp_w_hi_done"), sem("mlp_w_lo_done")
        self.y_in = sem("y_in")
        self.stats_done, self.aggr_done, self.var_done, self.rstd_done, self.y_ready = (
            sem("mlp_stats"), sem("mlp_aggr"), sem("mlp_var"), sem("mlp_rstd"), sem("y_ready"))
        self.yT_made, self.yT_hi_done, self.y32_done, self.yT_done = (
            sem("yT_made"), sem("yT_hi_done"), sem("y32_done"), sem("yT_done"))


    @staticmethod
    def stage_of(i):
        return i % 2 if i < 4 else i % 4

    def weight_piece(self, a, i):
        j, half = i // 4, i % 2
        if i % 4 < 2:
            return a["fc_w"].rearrange("(c p) n -> p c n", p=128)[:, 2 * half:2 * half + 2, D * j:D * (j + 1)]
        c = C * j + 2 * half
        return a["proj_w"].rearrange("(c p) n -> p c n", p=128)[:, c:c + 2, :]

    def load_piece(self, sp, a, i, stages):
        before = [k for k in range(i) if self.stage_of(k) == self.stage_of(i)]
        if before:
            sp.wait_ge(self.w_lo_done, before[-1] + 1)
        sp.dma_start(stages[self.stage_of(i)], self.weight_piece(a, i)).then_inc(self.w_in[self.stage_of(i)], 16)

    def split_hi(self, act, i, hi, stages):
        act.wait_ge(self.w_in[self.stage_of(i)], 16 * sum(self.stage_of(k) == self.stage_of(i) for k in range(i + 1)))
        act.copy(hi[:, 2 * (i % 2):2 * (i % 2) + 2, :], stages[self.stage_of(i)]).then_inc(self.w_hi_done, 1)

    def split_lo(self, dve, i, hi, lo, stages):
        c = slice(2 * (i % 2), 2 * (i % 2) + 2)
        dve.wait_ge(self.w_hi_done, i + 1)
        dve.tensor_tensor(lo[:, c, :], stages[self.stage_of(i)], hi[:, c, :].bitcast(F32), ALU.subtract).then_inc(self.w_lo_done, 1)


    def load_rows(self, sp, hidden, g):
        src = hidden.rearrange("(g m) t d -> g t m d", m=MG)
        sp.dma_start(self.y, src[bass.ds(g, 1), :, :, :].rearrange("o t m d -> t (o m) d")).then_inc(self.y_in, 16)

    def row_stats(self, dve, g, i):
        if i == 0:
            dve.wait_ge(self.y_in, 16 * (g + 1))
        dve.bn_stats(self.st[:, i, :], self.y[:, i, :]).then_inc(self.stats_done, 1)

    def row_aggr(self, dve, g):
        dve.wait_ge(self.stats_done, MG * (g + 1))
        dve.memset(self.after_stats[:, :], 0.0)
        for i in range(MG):
            dve.bn_aggr(self.mv[:, i, :], self.st[:, i, :]).then_inc(self.aggr_done, 1)

    def row_rstd(self, pool, g):
        pool.wait_ge(self.aggr_done, MG * (g + 1))
        pool.tensor_tensor(self.ve[:, :], self.mv[:, :, 1], self.eps[0:T, :].broadcast_to([T, MG]), ALU.add).then_inc(self.var_done, 1)
        pool.wait_ge(self.var_done, g + 1)
        pool.tensor_tensor(self.rs[:, :], self.ve[:, :], self.minus_half[0:T, :].broadcast_to([T, MG]), ALU.pow).then_inc(self.rstd_done, 1)

    def row_scale(self, dve, g, i):
        if i == 0:
            dve.wait_ge(self.rstd_done, g + 1)
        dve.tensor_scalar(self.y[:, i, :], self.y[:, i, :], self.mv[:, i, 0:1], self.rs[:, i:i + 1], ALU.subtract, ALU.mult).then_inc(self.y_ready, 1)


    def turn(self, pe, bank, g, c):
        if c == 0:
            pe.wait_ge(self.y_ready, MG * (g + 1))
        for i in range(MG):
            last = pe.transpose(bank[:, i * T:(i + 1) * T], self.y[:, i, c * 128:(c + 1) * 128], self.ident[0:T, 0:T])
        last.then_inc(self.yT_made, 1)

    def turned_to_hi(self, act, bank, g, c):
        act.wait_ge(self.yT_made, C * g + c + 1)
        act.activation(self.turned_hi[:, c, :], bank[:, 0:MG * T], ACT.Identity, bias=self.ln_b[:, c:c + 1], scale=self.ln_g[:, c:c + 1]).then_inc(self.yT_hi_done, 1)

    def turned_to_32(self, dve, bank, g, c):
        dve.wait_ge(self.yT_hi_done, C * g + c + 1)
        at_least(dve, self.yT_done, C * g + c - 1)
        dve.tensor_scalar(self.turned32[:, c % 2, :], bank[:, 0:MG * T], self.ln_g[:, c:c + 1], self.ln_b[:, c:c + 1], ALU.mult, ALU.add).then_inc(self.y32_done, 1)

    def turned_to_lo(self, pool, g, c):
        pool.wait_ge(self.y32_done, C * g + c + 1)
        pool.tensor_tensor(self.turned_lo[:, c, :], self.turned32[:, c % 2, :], self.turned_hi[:, c, :].bitcast(F32), ALU.subtract).then_inc(self.yT_done, 1)


def mlp(nc, a, hidden, out, m):
    with ExitStack() as ctx:
        def sb(name, shape, dt=F32):
            return ctx.enter_context(nc.sbuf_tensor(name, shape, dt))

        def sem(name):
            return ctx.enter_context(nc.semaphore(name))

        WP = 4 * C
        N = MG * T
        w_hi = [m.w_hi[x] for x in WN] + [sb(f"w{i}_hi", [128, C, D], F32R) for i in range(4, 2 * C)]
        w_lo = [m.w_lo[x] for x in WN] + [sb(f"w{i}_lo", [128, C, D], F32R) for i in range(4, 2 * C)]
        more_stage = sb("more_stage", [128, 2, C // 2, D])
        stages = [half for both in (m.stage, more_stage) for half in (both[:, 0, :, :], both[:, 1, :, :])]
        res = sb("mlp_res", [T, MG, D])
        h32 = sb("h32", [128, 2, N])
        h_hi, h_lo = sb("h_hi", [128, 2, N], F32R), sb("h_lo", [128, 2, N], F32R)
        down32 = sb("down32", [128, C, N])
        turned = ctx.enter_context(nc.psum_tensor("mlp_turned", [128, 2, 512], F32))
        up = ctx.enter_context(nc.psum_tensor("mlp_up", [128, 2, 512], F32))
        down = ctx.enter_context(nc.psum_tensor("mlp_down", [128, C, 512], F32))

        res_in, stored = sem("mlp_res_in"), sem("stored")
        up_made, gelu_done, h_hi_done, h_done, down_made = (
            sem("up_made"), sem("gelu_done"), sem("h_hi_done"), sem("h_done"), sem("down_made"))
        down32_by_act, down32_by_dve, back_made, out_done = (
            sem("down32_by_act"), sem("down32_by_dve"), sem("back_made"), sem("out_done"))

        block = ctx.enter_context(nc.Block())

        def groups(eng, body):
            body(0, True)
            with eng.Fori(1, NG - 1) as i:
                body(i, True)
            body(NG - 1)

        def first(g):
            return isinstance(g, int) and g == 0

        def split_at(g, k):
            if not first(g) or k >= FC - C:
                return ()
            return {1: (k + 3, k + 4), 2: (k + 4, k + 5)}.get(k % C, ())

        @block.sync
        def _(sp):
            dst = out.rearrange("(g m) t d -> g t m d", m=MG)
            hid = hidden.rearrange("(g m) t d -> g t m d", m=MG)

            def load_residual(g):
                sp.dma_start(res[:, :, :], hid[bass.ds(g, 1), :, :, :].rearrange("o t m d -> t (o m) d")).then_inc(res_in, 16)

            def store(g):
                sp.wait_ge(out_done, MG * (g + 1))
                sp.dma_start(dst[bass.ds(g, 1), :, :, :].rearrange("o t m d -> t (o m) d"), res[:, :, :]).then_inc(stored, 16)

            def body(g, more=False):
                if more:
                    sp.wait_ge(m.yT_made, C * (g + 1))
                    m.load_rows(sp, hidden, g + 1)
                if first(g):
                    for i in range(8, WP):
                        m.load_piece(sp, a, i, stages)
                if more:
                    store(g)
                    sp.wait_ge(stored, 16 * (g + 1))
                    load_residual(g + 1)
                else:
                    for i in range(MG):
                        sp.wait_ge(out_done, MG * g + i + 1)
                        sp.dma_start(out[MG * g + i, :, :], res[:, i, :]).then_inc(stored, 16)

            for i in range(4, 8):
                m.load_piece(sp, a, i, stages)
            sp.wait_ge(m.x_stored, 16 * NS)
            load_residual(0)
            groups(sp, body)
            sp.wait_ge(stored, 16 * (NG - 1 + MG))

        @block.gpsimd
        def _(pool):
            def body(g, more=False):
                if more:
                    m.row_rstd(pool, g + 1)
                    for c in range(C):
                        m.turned_to_lo(pool, g + 1, c)

            groups(pool, body)

        @block.scalar
        def _(act):
            def body(g, more=False):
                for k in range(FC):
                    act.wait_ge(up_made, FC * g + k + 1)
                    at_least(act, h_done, FC * g + k - 1)
                    act.activation(h32[:, k % 2, :], up[:, k % 2, 0:N], ACT.Gelu_apprx_tanh, bias=m.f_bias[:, k:k + 1]).then_inc(gelu_done, 1)
                    act.wait_ge(gelu_done, FC * g + k + 1)
                    at_least(act, down_made, FC * g + k - 1)
                    act.copy(h_hi[:, k % 2, :], h32[:, k % 2, :]).then_inc(h_hi_done, 1)
                    for i in split_at(g, k):
                        m.split_hi(act, i, w_hi[i // 2], stages)
                if more:
                    for c in range(C):
                        if c == 0:
                            act.wait_ge(up_made, FC * (g + 1))
                        m.turned_to_hi(act, turned[:, c % 2, :], g + 1, c)
                act.wait_ge(down_made, FC * (g + 1))
                at_least(act, back_made, MG * g)
                for c in (0, 1):
                    act.activation(down32[:, c, :], down[:, c, 0:N], ACT.Identity, bias=m.p_bias[:, c:c + 1]).then_inc(down32_by_act, 1)

            for i in (2, 3):
                m.split_hi(act, i, w_hi[i // 2], stages)
            groups(act, body)

        @block.vector
        def _(dve):
            def result(g, rows):
                for i in rows:
                    dve.wait_ge(back_made, MG * g + i + 1)
                    if i == 0:
                        dve.wait_ge(res_in, 16 * (g + 1))
                    dve.tensor_tensor(res[:, i, :], turned[0:T, i % 2, :], res[:, i, :], ALU.add).then_inc(out_done, 1)

            def body(g, more=False):
                for k in range(FC):
                    if k < 2 and not first(g):
                        result(g - 1, (2 * k, 2 * k + 1))
                    dve.wait_ge(h_hi_done, FC * g + k + 1)
                    dve.tensor_tensor(h_lo[:, k % 2, :], h32[:, k % 2, :], h_hi[:, k % 2, :].bitcast(F32), ALU.subtract).then_inc(h_done, 1)
                    for i in split_at(g, k):
                        m.split_lo(dve, i, w_hi[i // 2], w_lo[i // 2], stages)
                    if more and 4 <= k < 4 + MG:
                        m.row_stats(dve, g + 1, k - 4)
                    if more and k == 8:
                        m.row_aggr(dve, g + 1)
                    if more and 10 <= k < 10 + MG:
                        m.row_scale(dve, g + 1, k - 10)
                if more:
                    for c in range(C):
                        m.turned_to_32(dve, turned[:, c % 2, :], g + 1, c)
                dve.wait_ge(down_made, FC * (g + 1))
                at_least(dve, back_made, MG * g)
                for c in (2, 3):
                    dve.tensor_scalar(down32[:, c, :], down[:, c, 0:N], m.p_bias[:, c:c + 1], None, ALU.add).then_inc(down32_by_dve, 1)
                if not more:
                    result(g, range(MG))

            for i in (2, 3):
                m.split_lo(dve, i, w_hi[i // 2], w_lo[i // 2], stages)
            groups(dve, body)

        @block.tensor
        def _(pe):
            def project_up(g, k):
                if k % C == 0:
                    pe.wait_ge(m.w_lo_done, k + 2)
                at_least(pe, gelu_done, FC * g + k - 1)
                hi, lo, f = w_hi[2 * (k // C)], w_lo[2 * (k // C)], slice(k % C * 128, (k % C + 1) * 128)
                todo = [xy for c in range(C) for xy in ((hi[:, c, f], m.turned_hi[:, c, :]), (hi[:, c, f], m.turned_lo[:, c, :]), (lo[:, c, f], m.turned_hi[:, c, :]))]
                for i, (w, v) in enumerate(todo):
                    if k == 0 and i % 3 == 0:
                        pe.wait_ge(m.yT_done, C * g + i // 3 + 1)
                    last = pe.matmul(up[:, k % 2, 0:N], w, v, start=i == 0, stop=i == len(todo) - 1)
                last.then_inc(up_made, 1)

            def project_down(g, j):
                pe.wait_ge(h_done, FC * g + j + 1)
                if j % C == 0:
                    pe.wait_ge(m.w_lo_done, j + 4)
                hi, lo = w_hi[2 * (j // C) + 1], w_lo[2 * (j // C) + 1]
                for c in range(C):
                    if j == 0 and c in (0, 2):
                        at_least(pe, (down32_by_act, down32_by_dve)[c // 2], 2 * g)
                    f = slice(c * 128, (c + 1) * 128)
                    for e, (w, v) in enumerate(((hi, h_hi), (hi, h_lo), (lo, h_hi))):
                        last = pe.matmul(down[:, c, 0:N], w[:, j % C, f], v[:, j % 2, :], start=j == 0 and e == 0, stop=j == FC - 1 and e == 2)
                last.then_inc(down_made, 1)

            def turn_back(g, rows):
                for i in rows:
                    if i == 0:
                        pe.wait_ge(down32_by_act, 2 * (g + 1))
                        pe.wait_ge(down32_by_dve, 2 * (g + 1))
                    if i >= 2:
                        pe.wait_ge(out_done, MG * g + i - 1)
                    for c in range(C):
                        last = pe.transpose(turned[0:T, i % 2, c * 128:(c + 1) * 128], down32[:, c, i * T:(i + 1) * T], m.ident[:, :])
                    last.then_inc(back_made, 1)

            def body(g, more=False):
                for k in range(FC + 1):
                    if k < FC:
                        project_up(g, k)
                    if k < 2 and not first(g):
                        turn_back(g - 1, (2 * k, 2 * k + 1))
                    if more and k >= FC - 1:
                        for c in (0, 1) if k < FC else (2, 3):
                            if c < 2:
                                at_least(pe, out_done, MG * g)
                            else:
                                pe.wait_ge(m.y32_done, C * (g + 1) + c - 1)
                            m.turn(pe, turned[:, c % 2, :], g + 1, c)
                    if k >= 1:
                        project_down(g, k - 1)
                if not more:
                    turn_back(g, range(MG))

            groups(pe, body)


def build(nc, a, out):
    hidden = nc.dram_tensor("hidden", [B, T, D], F32, kind="Internal").ap()
    with ExitStack() as ctx:
        m = Mlp(nc, ctx)
        with nc.Block() as block:
            @block.gpsimd
            def _(pool):
                pool.memset(m.ident[:, :], 0.0).then_inc(m.ident_ready, 1)
                pool.wait_ge(m.ident_ready, 1)
                pool.affine_select(out=m.ident[:, :], in_=m.ident[:, :], compare_op=ALU.not_equal, fill=1.0, base=0,
                                   pattern=[[-1, 128]], channel_multiplier=1).then_inc(m.ident_ready, 1)
        attention_layers(nc, a, hidden, m)
        mlp(nc, a, hidden, out, m)


def kernel(x, ctx_2048, mask_BxS2_bf1, **w):
    import numpy as np
    import concourse.bacc as bacc
    from concourse.bass_utils import run_bass_kernel_spmd

    ctx = np.zeros((B, SP, D), np.float32)
    ctx[:, :S, :] = np.asarray(ctx_2048)
    l0, l1 = "L0_xattn_", "L1_xattn_"

    def columns(v):
        return np.asarray(v).reshape(-1, 128).T

    def by_dim(v):
        v = np.asarray(v)
        return v.reshape(-1, G, GH, HD).transpose(0, 1, 3, 2).reshape(v.shape)

    named = {
        "x": x, "ctx": ctx.reshape(B, KT, KR, D), "mask": np.asarray(mask_BxS2_bf1).view(np.uint8),
        "w0q": by_dim(np.asarray(w[l0 + "Wq"]).T), "w0k": by_dim(np.asarray(w[l0 + "Wk"]).T), "w0v": np.asarray(w[l0 + "Wv"]).T,
        "w0o": np.asarray(w[l0 + "Wo"]).T, "g0": columns(w[l0 + "ln_gamma"]), "b0": columns(w[l0 + "ln_beta"]), "gate": w[l0 + "gate"],
        "w1q": by_dim(w[l1 + "q_w"]), "w1k": by_dim(w[l1 + "k_w"]), "w1v": w[l1 + "v_w"], "w1o": w[l1 + "cproj_w"],
        "ln1_w": w[l1 + "ln1_w"], "ln1_b": w[l1 + "ln1_b"], "q_b": by_dim(w[l1 + "q_b"]), "k_b": columns(by_dim(w[l1 + "k_b"])), "v_b": columns(w[l1 + "v_b"]),
        "cproj_b": w[l1 + "cproj_b"], "ln2_w": columns(w[l1 + "ln2_w"]), "ln2_b": columns(w[l1 + "ln2_b"]), "fc_w": w[l1 + "fc_w"],
        "fc_b": columns(w[l1 + "fc_b"]), "proj_w": w[l1 + "proj_w"], "proj_b": columns(w[l1 + "proj_b"]),
    }
    nc = bacc.Bacc("TRN2", target_bir_lowering=False, num_devices=1)
    arrays, a = {}, {}
    for name, value in named.items():
        value = np.ascontiguousarray(value)
        arrays[f"in_{name}"] = value
        a[name] = nc.dram_tensor(f"in_{name}", value.shape, mybir.dt.from_np(value.dtype), kind="ExternalInput").ap()
    out = nc.dram_tensor("out", [B, T, D], F32, kind="ExternalOutput").ap()
    build(nc, a, out)
    r = run_bass_kernel_spmd(nc, [arrays], core_ids=[0])
    return r.results[0]["out"]
```
